# Optimizing a Trainium2 kernel written in Bass

```python
import numpy as np
import jax
import jax.numpy as jnp

def _softmax(x, axis=-1):
    return jax.nn.softmax(x, axis=axis)

def _gelu(x):
    return jax.nn.gelu(x, approximate=True)

def _silu(x):
    return jax.nn.silu(x)

def _sigmoid(x):
    return jax.nn.sigmoid(x)

def _layernorm(x, axis=-1, eps=1e-05):
    m = jnp.mean(x, axis=axis, keepdims=True)
    v = jnp.var(x, axis=axis, keepdims=True)
    return (x - m) / jnp.sqrt(v + eps)

def _scatter_add(tgt, idx, src, axis=0):
    return tgt.at[idx].add(src)

def _segment_sum(src, seg, n):
    return jax.ops.segment_sum(src, seg, n)
kernel_name = 'mk_cond_resid_d4_seqx_r8_9d43b2'

def setup_inputs(seed: int=0):
    np.random.seed(seed)
    _w = jnp.asarray

    def _rec_inputs():
        import jax
        import jax.numpy as jnp
        _rk = jax.random.key(seed)
        x = 7.22e-05 + 1 * jax.random.normal(jax.random.fold_in(_rk, 1), (2, 512, 128), jnp.float32)
        _lenS = 512 - jax.random.randint(jax.random.fold_in(_rk, 7), (2,), 0, max(1, 512 // 4) + 1, jnp.int32)
        _lenS2 = 512 - jax.random.randint(jax.random.fold_in(_rk, 8), (2,), 0, max(1, 512 // 4) + 1, jnp.int32)
        cond_8 = -0.104238 + 1.01173 * jax.random.normal(jax.random.fold_in(_rk, 11), (2, 8), jnp.float32)
        return (x, cond_8)
    x, cond_8 = _rec_inputs()

    def _L0_cond_setup():
        import jax, jax.numpy as jnp
        import numpy as np
        TOP_K = 2
        NUM_MOE_LAYERS = 12

        def _gemma_mlp(x, gate_w, up_w, down_w):
            g = jnp.einsum('bsh,hi->bsi', x, gate_w)
            u = jnp.einsum('bsh,hi->bsi', x, up_w)
            return jnp.einsum('bsi,ih->bsh', jax.nn.gelu(g, approximate=True) * u, down_w)
        key = jax.random.key(seed)
        ks = jax.random.split(key, 8)
        B, S, H, I, E = (32, 32, 128, 512, 8)
        std = 0.02
        return {'x': jax.random.normal(ks[0], (B, S, H), jnp.float32), 'router_logits': jax.random.normal(ks[1], (B, E), jnp.float32), 'skill_gate': jax.random.normal(ks[2], (E, H, I), jnp.float32) * std, 'skill_up': jax.random.normal(ks[3], (E, H, I), jnp.float32) * std, 'skill_down': jax.random.normal(ks[4], (E, I, H), jnp.float32) * std, 'shared_gate': jax.random.normal(ks[5], (H, I), jnp.float32) * std, 'shared_up': jax.random.normal(ks[6], (H, I), jnp.float32) * std, 'shared_down': jax.random.normal(ks[7], (I, H), jnp.float32) * std}
    _L0_cond_all = _L0_cond_setup()
    _L0_cond_in = {k: v for k, v in _L0_cond_all.items() if k in ('skill_gate', 'skill_up', 'skill_down', 'shared_gate', 'shared_up', 'shared_down')}
    del _L0_cond_all

    def _L1_cond_setup():
        import jax, jax.numpy as jnp
        import numpy as np
        R = 16
        ALPHA = 32.0
        SCALING = ALPHA / R
        key = jax.random.key(seed)
        ks = jax.random.split(key, 6)
        B, T, C, O, E = (16, 1500, 128, 128, 8)
        x = jax.random.normal(ks[0], (B, T, C), dtype=jnp.float32)
        w = jax.random.uniform(ks[1], (B, E), dtype=jnp.float32)
        W_base = jax.random.normal(ks[2], (O, C), dtype=jnp.float32) * 0.02
        b_base = jax.random.normal(ks[3], (O,), dtype=jnp.float32) * 0.02
        As = jax.random.normal(ks[4], (E, R, C), dtype=jnp.float32) * 0.02
        Bs = jax.random.normal(ks[5], (E, O, R), dtype=jnp.float32) * 0.02
        return {'x': x, 'w': w, 'W_base': W_base, 'b_base': b_base, 'As': As, 'Bs': Bs}
    _L1_cond_all = _L1_cond_setup()
    _L1_cond_in = {k: v for k, v in _L1_cond_all.items() if k in ('W_base', 'b_base', 'As', 'Bs')}
    del _L1_cond_all

    def _L2_cond_setup():
        import jax, jax.numpy as jnp
        import numpy as np
        key = jax.random.key(seed)
        k1, k2, k3, k4, k5 = jax.random.split(key, 5)
        B, N, T, O, G = (32, 32, 128, 128, 8)
        x = jax.random.normal(k1, (B, N, T), dtype=jnp.float32)
        y = jax.random.uniform(k2, (B, G), dtype=jnp.float32)
        weight = jax.random.normal(k3, (G, O, T), dtype=jnp.float32) * (1.0 / np.sqrt(T))
        mask = jax.random.uniform(k4, (O, T), dtype=jnp.float32)
        bias = jax.random.normal(k5, (O,), dtype=jnp.float32)
        return {'x': x, 'y': y, 'weight': weight, 'mask': mask, 'bias': bias}
    _L2_cond_all = _L2_cond_setup()
    _L2_cond_in = {k: v for k, v in _L2_cond_all.items() if k in ('weight', 'mask', 'bias')}
    del _L2_cond_all

    def _L3_cond_setup():
        import jax, jax.numpy as jnp
        import numpy as np
        B, S, D = (16, 256, 128)
        E, H = (8, 256)
        key = jax.random.key(seed)
        ks = jax.random.split(key, 8)
        scale = 0.02
        x = jax.random.normal(ks[0], (B, S, D), dtype=jnp.float32)
        opcode_onehot = jax.random.uniform(ks[1], (B, E), dtype=jnp.float32)
        W_up = jax.random.normal(ks[2], (E, H, D), dtype=jnp.float32) * scale
        b_up = jnp.zeros((E, H), dtype=jnp.float32)
        W_gate = jax.random.normal(ks[3], (E, H, D), dtype=jnp.float32) * scale
        b_gate = jnp.zeros((E, H), dtype=jnp.float32)
        W_down = jax.random.normal(ks[4], (E, D, H), dtype=jnp.float32) * scale
        b_down = jnp.zeros((E, D), dtype=jnp.float32)
        return {'x': x, 'opcode_onehot': opcode_onehot, 'W_up': W_up, 'b_up': b_up, 'W_gate': W_gate, 'b_gate': b_gate, 'W_down': W_down, 'b_down': b_down}
    _L3_cond_all = _L3_cond_setup()
    _L3_cond_in = {k: v for k, v in _L3_cond_all.items() if k in ('W_up', 'b_up', 'W_gate', 'b_gate', 'W_down', 'b_down')}
    del _L3_cond_all
    return {'x': x, 'cond_8': cond_8, 'L0_cond_skill_gate': _L0_cond_in['skill_gate'], 'L0_cond_skill_up': _L0_cond_in['skill_up'], 'L0_cond_skill_down': _L0_cond_in['skill_down'], 'L0_cond_shared_gate': _L0_cond_in['shared_gate'], 'L0_cond_shared_up': _L0_cond_in['shared_up'], 'L0_cond_shared_down': _L0_cond_in['shared_down'], 'L1_cond_W_base': _L1_cond_in['W_base'], 'L1_cond_b_base': _L1_cond_in['b_base'], 'L1_cond_As': _L1_cond_in['As'], 'L1_cond_Bs': _L1_cond_in['Bs'], 'L2_cond_weight': _L2_cond_in['weight'], 'L2_cond_mask': _L2_cond_in['mask'], 'L2_cond_bias': _L2_cond_in['bias'], 'L3_cond_W_up': _L3_cond_in['W_up'], 'L3_cond_b_up': _L3_cond_in['b_up'], 'L3_cond_W_gate': _L3_cond_in['W_gate'], 'L3_cond_b_gate': _L3_cond_in['b_gate'], 'L3_cond_W_down': _L3_cond_in['W_down'], 'L3_cond_b_down': _L3_cond_in['b_down']}

def reference(x, cond_8, L0_cond_skill_gate, L0_cond_skill_up, L0_cond_skill_down, L0_cond_shared_gate, L0_cond_shared_up, L0_cond_shared_down, L1_cond_W_base, L1_cond_b_base, L1_cond_As, L1_cond_Bs, L2_cond_weight, L2_cond_mask, L2_cond_bias, L3_cond_W_up, L3_cond_b_up, L3_cond_W_gate, L3_cond_b_gate, L3_cond_W_down, L3_cond_b_down):
    import jax
    import jax.numpy as jnp

    def _L0_cond_ref(x, router_logits, skill_gate, skill_up, skill_down, shared_gate, shared_up, shared_down):
        import jax, jax.numpy as jnp
        import numpy as np
        TOP_K = 2
        NUM_MOE_LAYERS = 12

        def _gemma_mlp(x, gate_w, up_w, down_w):
            g = jnp.einsum('bsh,hi->bsi', x, gate_w)
            u = jnp.einsum('bsh,hi->bsi', x, up_w)
            return jnp.einsum('bsi,ih->bsh', jax.nn.gelu(g, approximate=True) * u, down_w)
        B = x.shape[0]
        E = skill_gate.shape[0]
        rw = jax.nn.softmax(router_logits.astype(jnp.float32), axis=-1)
        w, sel = jax.lax.top_k(rw, TOP_K)
        w = w / w.sum(axis=-1, keepdims=True)
        w = w.astype(x.dtype)
        scale = 1.0 / NUM_MOE_LAYERS
        w = scale * w + (1.0 - scale) * jax.lax.stop_gradient(w)
        dense_w = jnp.zeros((B, E), x.dtype).at[jnp.arange(B)[:, None], sel].add(w)

        def step(acc, params):
            g, u, d, we = params
            return (acc + we[:, None, None] * _gemma_mlp(x, g, u, d), None)
        out, _ = jax.lax.scan(step, jnp.zeros_like(x), (skill_gate, skill_up, skill_down, dense_w.T))
        out = out + _gemma_mlp(x, shared_gate, shared_up, shared_down)
        return out

    def _L1_cond_ref(x, w, W_base, b_base, As, Bs):
        import jax, jax.numpy as jnp
        import numpy as np
        R = 16
        ALPHA = 32.0
        SCALING = ALPHA / R
        out = jnp.einsum('btc,oc->bto', x, W_base) + b_base
        h = jnp.einsum('btc,erc->bter', x, As)
        lora = jnp.einsum('bter,eor,be->bto', h, Bs, w)
        return out + lora * SCALING

    def _L2_cond_ref(x, y, weight, mask, bias):
        import jax, jax.numpy as jnp
        import numpy as np
        masked_w = weight * mask[None, :, :]
        w_bot = jnp.einsum('bg,got->bot', y, masked_w)
        return jnp.einsum('bnt,bot->bno', x, w_bot) + bias

    def _L3_cond_ref(x, opcode_onehot, W_up, b_up, W_gate, b_gate, W_down, b_down):
        import jax, jax.numpy as jnp
        import numpy as np
        B, S, D = (16, 256, 128)
        E, H = (8, 256)
        expert = jnp.argmax(opcode_onehot, axis=-1)
        wu, bu = (W_up[expert], b_up[expert])
        wg, bg = (W_gate[expert], b_gate[expert])
        wd, bd = (W_down[expert], b_down[expert])
        up = jnp.einsum('bsd,bhd->bsh', x, wu) + bu[:, None, :]
        gate = jnp.einsum('bsd,bhd->bsh', x, wg) + bg[:, None, :]
        hidden = jax.nn.silu(up) * gate
        out = jnp.einsum('bsh,bdh->bsd', hidden, wd) + bd[:, None, :]
        return out
    x = x + _L0_cond_ref(x, cond_8, L0_cond_skill_gate, L0_cond_skill_up, L0_cond_skill_down, L0_cond_shared_gate, L0_cond_shared_up, L0_cond_shared_down)
    x = x + _L1_cond_ref(x, cond_8, L1_cond_W_base, L1_cond_b_base, L1_cond_As, L1_cond_Bs)
    x = x + _L2_cond_ref(x, cond_8, L2_cond_weight, L2_cond_mask, L2_cond_bias)
    x = x + _L3_cond_ref(x, cond_8, L3_cond_W_up, L3_cond_b_up, L3_cond_W_gate, L3_cond_b_gate, L3_cond_W_down, L3_cond_b_down)
    return x

_drawn_inputs = setup_inputs


def setup_inputs(seed=0):
    import zlib

    import numpy as np

    out = dict(_drawn_inputs(seed))
    spreads = {'L3_cond_b_up': (0.0, 0.8), 'L3_cond_b_gate': (0.0, 0.8), 'L3_cond_b_down': (0.0, 0.8)}
    factors = {'L0_cond_skill_gate': 7.347,
     'L0_cond_skill_up': 7.26,
     'L0_cond_skill_down': 7.227,
     'L0_cond_shared_gate': 5.24,
     'L0_cond_shared_up': 5.127,
     'L0_cond_shared_down': 5.122,
     'L1_cond_b_base': 13.425}
    for name, (base, spread) in spreads.items():
        noise = np.random.default_rng([zlib.crc32(name.encode()), seed]).standard_normal(out[name].shape)
        drawn = base * np.exp(spread * noise) if base else spread * noise
        out[name] = jnp.asarray(drawn.astype(out[name].dtype))
    for name, factor in factors.items():
        out[name] = (out[name] * factor).astype(out[name].dtype)
    return out
```

```python
import concourse.bass as bass
from concourse import mybir
from contextlib import ExitStack


def build(nc, x, cond, sk_gate, sk_up, sk_down, sh_gate, sh_up, sh_down, W_base, b_base, As, Bs,
          weight, mask, bias, W_up, b_up, W_gate, b_gate, W_down, b_down, out):
    F32, F32R, U32 = mybir.dt.float32, mybir.dt.float32r, mybir.dt.uint32
    ALU, ACT = mybir.AluOpType, mybir.ActivationFunctionType

    B, S, D = x.shape
    E, _, I = sk_gate.shape
    R = As.shape[1]
    H = W_up.shape[1]
    P = 128
    J = S // P
    C = I // P
    HC = H // P
    TOP = 2
    LORA_SCALE = 32.0 / R
    ROUTE_SCALE = 1.0 / 12
    assert D == P and E * R == P and E == 8

    BLOCKS = [(0, 0), (0, 1)] + [(1 + TOP * b + k, b) for b in range(B) for k in range(TOP)]
    SETS = 1 + TOP * B
    STEPS = len(BLOCKS) * C
    FIRST_STEPS = (B + TOP) * C
    LAG = 2
    GATE, UP, DOWN = range(3)
    RING = 3

    TAIL = [(0, 0, S), (1, 0, S)]

    ctx = ExitStack()
    with ctx:
        def sb(name, shape, dt=F32):
            return ctx.enter_context(nc.sbuf_tensor(name, shape, dt))

        def ps(name):
            return ctx.enter_context(nc.psum_tensor(name, [P, 512], F32))

        def sem(name):
            return ctx.enter_context(nc.semaphore(name))

        ident = sb("ident", [P, P])
        ident_r = sb("ident_r", [P, P], F32R)
        cond_all = sb("cond_all", [P, B, E])
        top_val = sb("top_val", [P, B, 8])
        top_idx = sb("top_idx", [P, B, 8], U32)
        neg_max = sb("neg_max", [P, B])
        top_exp = sb("top_exp", [P, B, TOP])
        exp_sum = sb("exp_sum", [P, B, 1])
        exp_inv = sb("exp_inv", [P, B, 1])
        w_norm = sb("w_norm", [P, B, TOP])
        w_stop = sb("w_stop", [P, B, TOP])
        w_route = sb("w_route", [P, B, TOP])
        x_tok = sb("x_tok", [P, B, S])
        xT_hi = sb("xT_hi", [P, B, S], F32R)
        xT_lo = sb("xT_lo", [P, B, S], F32R)
        w_raw = sb("w_raw", [P, SETS, 3, I])
        w_hi = sb("w_hi", [P, SETS, 3, I], F32R)
        w_lo = sb("w_lo", [P, SETS, 3, I], F32R)
        gelu = sb("gelu", [P, 2, S])
        hid = sb("hid", [P, RING, S])
        hid_hi = sb("hid_hi", [P, RING, S], F32R)
        hid_lo = sb("hid_lo", [P, RING, S], F32R)
        base_sb = sb("base_sb", [P, P])
        base_id = sb("base_id", [P, P])
        b1_col = sb("b1_col", [P, 1])
        b1_wide = sb("b1_wide", [P, P])
        as_sb = sb("as_sb", [P, P])
        bs_sb = sb("bs_sb", [P, E, R])
        bs_mix = sb("bs_mix", [P, B, E, R])
        bsT = sb("bsT", [P, B, P])
        mix_w = sb("mix_w", [P, E, P])
        mask_sb = sb("mask_sb", [P, P])
        b2_col = sb("b2_col", [P, 1])
        mix_acc = sb("mix_acc", [P, B, P])
        mix_masked = sb("mix_masked", [P, B, P])
        A1T = sb("A1T", [P, B, P])
        A2 = sb("A2", [P, B, P])
        QT = sb("QT", [P, B, P])
        Q_hi = sb("Q_hi", [P, B, P], F32R)
        Q_lo = sb("Q_lo", [P, B, P], F32R)
        cb_col = sb("cb_col", [P, B])
        upgate_raw = sb("upgate_raw", [P, B, 2 * HC, P])
        down_raw = sb("down_raw", [P, B, P, HC])
        bug_col = sb("bug_col", [P, B, 2, HC])
        row_bias = sb("row_bias", [P, B, 2, P])
        row_sum = sb("row_sum", [P, B, P])
        out_bias = sb("out_bias", [P, B, P])
        upgateT = sb("upgateT", [P, B, 2 * HC * P])
        downT_hi = sb("downT_hi", [P, B, HC, P], F32R)
        downT_lo = sb("downT_lo", [P, B, HC, P], F32R)
        R_hi = sb("R_hi", [P, B, 2 * HC * P], F32R)
        R_lo = sb("R_lo", [P, B, 2 * HC * P], F32R)
        ug_bias = sb("ug_bias", [P, B, 2 * HC])
        x1_hi = sb("x1_hi", [P, B, S], F32R)
        x1_lo = sb("x1_lo", [P, B, S], F32R)
        silu = sb("silu", [P, HC, S])
        hid3 = sb("hid3", [P, HC, S])
        hid3_hi = sb("hid3_hi", [P, HC, S], F32R)
        hid3_lo = sb("hid3_lo", [P, HC, S], F32R)
        result = sb("result", [P, B, S])

        gate_ps = [ps("gate_ps0"), ps("gate_ps1")]
        up_ps = [ps("up_ps0"), ps("up_ps1")]
        acc_ps = [ps("acc_ps0"), ps("acc_ps1")]
        work_ps = [ps("work_ps0"), ps("work_ps1")]

        cond_in = sem("cond_in")
        x_in = [sem(f"x_in{b}") for b in range(B)]
        w_in = [[sem(f"w_in{s}_{m}") for m in range(3)] for s in range(SETS)]
        l1_in, l2_in = sem("l1_in"), sem("l2_in")
        l3_in = [sem(f"l3_in{b}") for b in range(B)]
        stored = [sem(f"stored{u}") for u in range(len(TAIL))]
        ident_set, ident_ready = sem("ident_set"), sem("ident_ready")
        bs_mix_ready = sem("bs_mix_ready")
        base_ready, b1_wide_ready = sem("base_ready"), sem("b1_wide_ready")
        row_sum_ready = sem("row_sum_ready")
        top_found, neg_max_ready, top_exp_ready = sem("top_found"), sem("neg_max_ready"), sem("top_exp_ready")
        route_step = sem("route_step")
        xT_ready, xT_hi_ready, xT_lo_ready = sem("xT_ready"), sem("xT_hi_ready"), sem("xT_lo_ready")
        w_hi_ready = [sem(f"w_hi_ready{s}") for s in range(SETS)]
        w_lo_ready = [sem(f"w_lo_ready{s}") for s in range(SETS)]
        gate_ready, up_ready, down_done = sem("gate_ready"), sem("up_ready"), sem("down_done")
        gelu_ready, hid_ready = sem("gelu_ready"), sem("hid_ready")
        hid_hi_ready, hid_lo_ready = sem("hid_hi_ready"), sem("hid_lo_ready")
        mix_step, masked_ready = sem("mix_step"), sem("masked_ready")
        prep_mm = sem("prep_mm")
        bsT_ready, A2_ready, A1T_ready = sem("bsT_ready"), sem("A2_ready"), sem("A1T_ready")
        QT_ready, Q_hi_ready, Q_lo_ready = sem("QT_ready"), sem("Q_hi_ready"), sem("Q_lo_ready")
        cb_ready, out_bias_ready = sem("cb_ready"), sem("out_bias_ready")
        upgateT_ready = sem("upgateT_ready")
        downT_hi_ready, downT_lo_ready = sem("downT_hi_ready"), sem("downT_lo_ready")
        R_hi_ready, R_lo_ready = sem("R_hi_ready"), sem("R_lo_ready")
        ug_bias_ready = sem("ug_bias_ready")
        acc_ready = sem("acc_ready")
        x1_hi_ready, x1_lo_ready = sem("x1_hi_ready"), sem("x1_lo_ready")
        up3_ready, gate3_ready = sem("up3_ready"), sem("gate3_ready")
        silu_ready, hid3_ready = sem("silu_ready"), sem("hid3_ready")
        hid3_hi_ready, hid3_lo_ready = sem("hid3_hi_ready"), sem("hid3_lo_ready")
        out_ready, result_ready = sem("out_ready"), sem("result_ready")

        (ST_AB, ST_A1, ST_Q, ST_BIAS, ST_UGT0, ST_UGT1, ST_DNT, ST_R0, ST_R1, ST_UGB) = range(10)

        def f32(ap):
            return ap.bitcast(F32)

        def step_parts(n):
            s, b = BLOCKS[n // C]
            return s, b, n % C

        def tail_banks(u, c):
            if u == 0:
                return work_ps[0], work_ps[1], acc_ps[0]
            return gate_ps[c], up_ps[c], work_ps[u - 1]

        block = ctx.enter_context(nc.Block())

        @block.sync
        def _(sp):
            sp.dma_start(cond_all[:, :, :], cond.rearrange("b e -> (b e)").partition_broadcast(P)).then_inc(cond_in, 16)
            for m, w in ((GATE, sh_gate), (UP, sh_up)):
                sp.dma_start(w_raw[:, 0, m, :], w).then_inc(w_in[0][m], 16)
            sp.dma_start(w_raw[:, 0, DOWN, :].rearrange("p (c h) -> p c h", c=C),
                         sh_down.rearrange("(c p) h -> p c h", p=P)).then_inc(w_in[0][DOWN], 16)

            def load_expert(s, e):
                one = bass.ds(e, 1)
                for m, w in ((GATE, sk_gate), (UP, sk_up)):
                    sp.dma_start(w_raw[:, s, m, :], w[one, :, :].rearrange("e h i -> h (e i)")).then_inc(w_in[s][m], 16)
                sp.dma_start(w_raw[:, s, DOWN, :].rearrange("p (c h) -> p c h", c=C),
                             sk_down[one, :, :].rearrange("e (c p) h -> p (e c) h", p=P)).then_inc(w_in[s][DOWN], 16)

            def load_l3(b, e):
                one = bass.ds(e, 1)
                for m, w in ((0, W_up), (1, W_gate)):
                    sp.dma_start(upgate_raw[:, b, m * HC:(m + 1) * HC, :],
                                 w[one, :, :].rearrange("e (p c) d -> p (e c) d", c=HC)).then_inc(l3_in[b], 16)
                sp.dma_start(down_raw[:, b, :, :],
                             W_down[one, :, :].rearrange("e d (p c) -> d (e p) c", c=HC)).then_inc(l3_in[b], 16)
                for m, v in ((0, b_up), (1, b_gate)):
                    sp.dma_start(bug_col[:, b, m, :],
                                 v[one, :].rearrange("e (p c) -> p (e c)", c=HC)).then_inc(l3_in[b], 16)
                sp.dma_start(row_bias[:, b, 1, :],
                             b_down[one, :].rearrange("e d -> (e d)").partition_broadcast(P)).then_inc(l3_in[b], 16)

            sp.wait_ge(top_found, B)
            first = [sp.value_load(top_idx[0:1, b, 0:1], min_val=0, max_val=E - 1) for b in range(B)]
            second = [sp.value_load(top_idx[0:1, b, 1:2], min_val=0, max_val=E - 1) for b in range(B)]
            load_expert(1, first[0])
            sp.dma_start(as_sb[:, :], As.rearrange("e r c -> (e r) c")).then_inc(l1_in, 16)
            sp.dma_start(bs_sb[:, :, :], Bs.rearrange("e o r -> o e r")).then_inc(l1_in, 16)
            sp.dma_start(base_sb[:, :], W_base).then_inc(l1_in, 16)
            sp.dma_start(mix_w[:, :, :], weight.rearrange("g o t -> o g t")).then_inc(l2_in, 16)
            sp.dma_start(mask_sb[:, :], mask).then_inc(l2_in, 16)
            load_expert(2, second[0])
            for b in range(B):
                sp.dma_start(row_bias[:, b, 0, :], bias.partition_broadcast(P)).then_inc(l3_in[b], 16)
                load_l3(b, first[b])
            load_expert(3, first[1])
            load_expert(4, second[1])
            for u, (b, lo, hi) in enumerate(TAIL):
                sp.wait_ge(result_ready, u + 1)
                tiles = slice(lo // P, hi // P)
                sp.dma_start(out[b, :, :].rearrange("(p j) d -> p j d", j=J)[:, tiles, :],
                             result[:, b, lo:hi].rearrange("p (j d) -> p j d", d=D)).then_inc(stored[u], 16)
            for u in range(len(TAIL)):
                sp.wait_ge(stored[u], 16)

        @block.gpsimd
        def _(pool):
            nc.gpsimd.memset(ident[:, :], 0.0).then_inc(ident_set, 1)
            pool.wait_ge(ident_set, 1)
            nc.gpsimd.affine_select(out=ident[:, :], in_=ident[:, :], compare_op=ALU.not_equal, fill=1.0, base=0,
                                    pattern=[[-1, P]], channel_multiplier=1).then_inc(ident_ready, 1)
            pool.wait_ge(ident_ready, 1)
            nc.gpsimd.tensor_copy(ident_r[:, :], ident[:, :]).then_inc(ident_ready, 1)

            def split_weight(s, m):
                pool.wait_ge(w_in[s][m], 16)
                nc.gpsimd.tensor_copy(w_hi[:, s, m, :], w_raw[:, s, m, :]).then_inc(w_hi_ready[s], 1)
                pool.wait_ge(w_hi_ready[s], m + 1)
                nc.gpsimd.tensor_tensor(w_lo[:, s, m, :], w_raw[:, s, m, :], f32(w_hi[:, s, m, :]),
                                        ALU.subtract).then_inc(w_lo_ready[s], 1)

            for m in range(3):
                split_weight(1, m)
            pool.wait_ge(l1_in, 16 * 4)
            pool.wait_ge(cond_in, 16)
            for b in range(B):
                nc.gpsimd.tensor_tensor(bs_mix[:, b, :, :], bs_sb[:, :, :],
                                        cond_all[:, b, :].unsqueeze(2).to_broadcast([P, E, R]),
                                        ALU.mult).then_inc(bs_mix_ready, 1)
            nc.gpsimd.tensor_tensor(base_id[:, :], base_sb[:, :], ident[:, :], ALU.add).then_inc(base_ready, 1)
            pool.wait_ge(l2_in, 16 * 3)
            nc.gpsimd.tensor_copy(b1_wide[:, :], b1_col[:, 0:1].to_broadcast([P, P])).then_inc(b1_wide_ready, 1)
            for m in range(3):
                split_weight(2, m)
            for b in range(B):
                pool.wait_ge(l3_in[b], 16 * 7)
            nc.gpsimd.tensor_tensor(row_sum[:, :, :], row_bias[:, :, 0, :], row_bias[:, :, 1, :],
                                    ALU.add).then_inc(row_sum_ready, 1)
            for s in range(3, SETS):
                for m in range(3):
                    split_weight(s, m)

        @block.scalar
        def _(act):
            for b in range(B):
                act.dma_start(x_tok[:, b, :], x[b, :, :].rearrange("(p j) d -> p (j d)", j=J)).then_inc(x_in[b], 16)
            with nc.allow_non_contiguous_dma(reason="2 x 128 single values"):
                act.dma_start(b1_col[:, :], b_base.rearrange("(o a) -> o a", a=1)).then_inc(l1_in, 16)
                act.dma_start(b2_col[:, :], bias.rearrange("(o a) -> o a", a=1)).then_inc(l2_in, 16)

            act.wait_ge(neg_max_ready, 1)
            for b in range(B):
                nc.scalar.activation(top_exp[:, b, :], top_val[:, b, 0:TOP], ACT.Exp,
                                     bias=neg_max[:, b:b + 1]).then_inc(top_exp_ready, 1)

            def split_x(b):
                act.wait_ge(xT_ready, b + 1)
                nc.scalar.activation(xT_hi[:, b, :], work_ps[b][:, :], ACT.Copy).then_inc(xT_hi_ready, 1)

            def split_shared(m):
                act.wait_ge(w_in[0][m], 16)
                nc.scalar.activation(w_hi[:, 0, m, :], w_raw[:, 0, m, :], ACT.Copy).then_inc(w_hi_ready[0], 1)

            split_x(0)
            split_shared(GATE)
            split_shared(UP)
            split_x(1)

            def prepare(n):
                if n == 8:
                    act.wait_ge(prep_mm, ST_Q + 1)
                    nc.scalar.activation(QT[:, :, :], work_ps[0][:, 0:B * P], ACT.Copy).then_inc(QT_ready, 1)
                    nc.scalar.activation(Q_hi[:, :, :], work_ps[0][:, B * P:2 * B * P],
                                         ACT.Copy).then_inc(Q_hi_ready, 1)
                if n in (10, 11):
                    act.wait_ge(prep_mm, (ST_UGT0, ST_UGT1)[n - 10] + 1)
                    nc.scalar.activation(upgateT[:, n - 10, :], work_ps[n - 10][:, :], ACT.Copy).then_inc(upgateT_ready, 1)
                if n == 12:
                    act.wait_ge(prep_mm, ST_DNT + 1)
                    nc.scalar.activation(downT_hi[:, :, :, :], work_ps[0][:, :], ACT.Copy).then_inc(downT_hi_ready, 1)
                if n in (13, 14):
                    act.wait_ge(prep_mm, (ST_R0, ST_R1)[n - 13] + 1)
                    nc.scalar.activation(R_hi[:, n - 13, :], work_ps[(n - 12) % 2][:, :], ACT.Copy).then_inc(R_hi_ready, 1)

            def split_x1(u):
                b, lo, hi = TAIL[u]
                if u == 0:
                    act.wait_ge(down_done, FIRST_STEPS)
                else:
                    act.wait_ge(acc_ready, u)
                nc.scalar.activation(x1_hi[:, b, lo:hi], acc_ps[b][:, lo:hi], ACT.Copy).then_inc(x1_hi_ready, 1)

            def tail_silu(u, c):
                b, lo, hi = TAIL[u]
                act.wait_ge(up3_ready, HC * u + c + 1)
                if u == 0:
                    act.wait_ge(ug_bias_ready, 1)
                else:
                    act.wait_ge(hid3_ready, HC)
                nc.scalar.activation(silu[:, c, lo:hi], tail_banks(u, c)[0][:, lo:hi], ACT.Silu,
                                     bias=ug_bias[:, b, c:c + 1]).then_inc(silu_ready, 1)

            def tail_hid_hi(u, c):
                b, lo, hi = TAIL[u]
                act.wait_ge(hid3_ready, HC * u + c + 1)
                if u:
                    act.wait_ge(out_ready, 1)
                nc.scalar.activation(hid3_hi[:, c, lo:hi], hid3[:, c, lo:hi], ACT.Copy).then_inc(hid3_hi_ready, 1)

            for n in range(STEPS):
                act.wait_ge(gate_ready, n + 1)
                if n >= 2:
                    act.wait_ge(hid_ready, n - 1)
                nc.scalar.activation(gelu[:, n % 2, :], gate_ps[n % 2][:, :], ACT.Gelu_apprx_tanh).then_inc(gelu_ready, 1)
                if n == 0:
                    split_shared(DOWN)
                prepare(n)
                act.wait_ge(hid_ready, n + 1)
                if n >= RING:
                    act.wait_ge(down_done, n - RING + 1)
                nc.scalar.activation(hid_hi[:, n % RING, :], hid[:, n % RING, :], ACT.Copy).then_inc(hid_hi_ready, 1)
                if n == 17:
                    split_x1(0)
                if n in (18, 19):
                    tail_silu(0, n - 18)
                if n in (19, 20):
                    tail_hid_hi(0, n - 19)
            for u in (1,):
                split_x1(u)
            for u in (1,):
                for c in range(HC):
                    tail_silu(u, c)
                for c in range(HC):
                    tail_hid_hi(u, c)

        @block.vector
        def _(dve):
            dve.wait_ge(cond_in, 16)
            for b in range(B):
                nc.vector.max(top_val[:, b, :], cond_all[:, b, :]).then_inc(route_step, 1)
            dve.wait_ge(route_step, B)
            for b in range(B):
                nc.vector.max_index(top_idx[:, b, :], top_val[:, b, :], cond_all[:, b, :]).then_inc(top_found, 1)
            nc.vector.tensor_scalar(neg_max[:, :], top_val[:, :, 0], -1.0, None, ALU.mult).then_inc(neg_max_ready, 1)

            def route_weights():
                dve.wait_ge(top_exp_ready, B)
                nc.vector.tensor_tensor(exp_sum[:, :, :], top_exp[:, :, 0:1], top_exp[:, :, 1:2],
                                        ALU.add).then_inc(route_step, 1)
                dve.wait_ge(route_step, B + 1)
                nc.vector.reciprocal(exp_inv[:, :, :], exp_sum[:, :, :]).then_inc(route_step, 1)
                dve.wait_ge(route_step, B + 2)
                nc.vector.tensor_tensor(w_norm[:, :, :], top_exp[:, :, :], exp_inv[:, :, :].to_broadcast([P, B, TOP]),
                                        ALU.mult).then_inc(route_step, 1)
                dve.wait_ge(route_step, B + 3)
                nc.vector.tensor_scalar(w_stop[:, :, :], w_norm[:, :, :], 1.0 - ROUTE_SCALE, None,
                                        ALU.mult).then_inc(route_step, 1)
                dve.wait_ge(route_step, B + 4)
                nc.vector.scalar_tensor_tensor(w_route[:, :, :], w_norm[:, :, :], ROUTE_SCALE, w_stop[:, :, :],
                                               ALU.mult, ALU.add).then_inc(route_step, 1)
                dve.wait_ge(route_step, B + 5)

            def split_x(b):
                dve.wait_ge(xT_hi_ready, b + 1)
                nc.vector.tensor_tensor(xT_lo[:, b, :], work_ps[b][:, :], f32(xT_hi[:, b, :]),
                                        ALU.subtract).then_inc(xT_lo_ready, 1)

            def split_shared(m):
                dve.wait_ge(w_hi_ready[0], m + 1)
                nc.vector.tensor_tensor(w_lo[:, 0, m, :], w_raw[:, 0, m, :], f32(w_hi[:, 0, m, :]),
                                        ALU.subtract).then_inc(w_lo_ready[0], 1)

            split_x(0)
            split_shared(GATE)
            split_shared(UP)
            split_x(1)

            def mix(g):
                for b in range(B):
                    y = cond_all[:, b, g:g + 1]
                    if g == 0:
                        dve.wait_ge(l2_in, 16 * 3)
                        op = nc.vector.tensor_scalar(mix_acc[:, b, :], mix_w[:, g, :], y, None, ALU.mult)
                    else:
                        dve.wait_ge(mix_step, B * (g - 1) + b + 1)
                        op = nc.vector.scalar_tensor_tensor(mix_acc[:, b, :], mix_w[:, g, :], y, mix_acc[:, b, :],
                                                            ALU.mult, ALU.add)
                    op.then_inc(mix_step, 1)

            def prepare(n):
                if n == 1:
                    route_weights()
                if n in (3, 4):
                    for g in range(E // 2 * (n - 3), E // 2 * (n - 2)):
                        mix(g)
                if n == 5:
                    dve.wait_ge(mix_step, B * E)
                    nc.vector.tensor_tensor(mix_masked[:, :, :], mix_acc[:, :, :],
                                            mask_sb[:, :].unsqueeze(1).to_broadcast([P, B, P]),
                                            ALU.mult).then_inc(masked_ready, 1)
                if n == 6:
                    dve.wait_ge(prep_mm, ST_AB + 1)
                    nc.vector.tensor_scalar(bsT[:, :, :], work_ps[0][:, 0:B * P].rearrange("p (b o) -> p b o", b=B),
                                            LORA_SCALE, None, ALU.mult).then_inc(bsT_ready, 1)
                    nc.vector.tensor_tensor(A2[:, :, :], work_ps[0][:, B * P:2 * B * P].rearrange("p (b o) -> p b o", b=B),
                                            ident[:, :].unsqueeze(1).to_broadcast([P, B, P]),
                                            ALU.add).then_inc(A2_ready, 1)
                if n == 7:
                    dve.wait_ge(prep_mm, ST_A1 + 1)
                    dve.wait_ge(base_ready, 1)
                    nc.vector.tensor_tensor(A1T[:, :, :], work_ps[1][:, 0:B * P].rearrange("p (b c) -> p b c", b=B),
                                            base_id[:, :].unsqueeze(1).to_broadcast([P, B, P]),
                                            ALU.add).then_inc(A1T_ready, 1)
                if n == 8:
                    dve.wait_ge(Q_hi_ready, 1)
                    nc.vector.tensor_tensor(Q_lo[:, :, :], work_ps[0][:, B * P:2 * B * P].rearrange("p (b d) -> p b d", b=B),
                                            f32(Q_hi[:, :, :]), ALU.subtract).then_inc(Q_lo_ready, 1)
                if n == 9:
                    dve.wait_ge(prep_mm, ST_BIAS + 1)
                    nc.vector.tensor_scalar(cb_col[:, :], work_ps[1][:, 0:B], b2_col[:, 0:1], None,
                                            ALU.add).then_inc(cb_ready, 1)
                    dve.wait_ge(row_sum_ready, 1)
                    nc.vector.tensor_tensor(out_bias[:, :, :], work_ps[1][:, P:P + B * P].rearrange("p (b d) -> p b d", b=B),
                                            row_sum[:, :, :], ALU.add).then_inc(out_bias_ready, 1)
                if n == 12:
                    dve.wait_ge(downT_hi_ready, 1)
                    nc.vector.tensor_tensor(downT_lo[:, :, :, :].rearrange("p b c d -> p (b c d)"), work_ps[0][:, :],
                                            f32(downT_hi[:, :, :, :].rearrange("p b c d -> p (b c d)")),
                                            ALU.subtract).then_inc(downT_lo_ready, 1)
                if n in (13, 14):
                    dve.wait_ge(R_hi_ready, n - 12)
                    nc.vector.tensor_tensor(R_lo[:, n - 13, :], work_ps[(n - 12) % 2][:, :], f32(R_hi[:, n - 13, :]),
                                            ALU.subtract).then_inc(R_lo_ready, 1)
                if n == 15:
                    dve.wait_ge(prep_mm, ST_UGB + 1)
                    nc.vector.tensor_tensor(ug_bias[:, :, :], work_ps[1][:, 0:B * 2 * HC].rearrange("p (b k) -> p b k", b=B),
                                            bug_col[:, :, :, :].rearrange("p b m c -> p b (m c)"),
                                            ALU.add).then_inc(ug_bias_ready, 1)

            def hid_low(n):
                dve.wait_ge(hid_hi_ready, n + 1)
                if n >= RING:
                    dve.wait_ge(down_done, n - RING + 1)
                nc.vector.tensor_tensor(hid_lo[:, n % RING, :], hid[:, n % RING, :], f32(hid_hi[:, n % RING, :]),
                                        ALU.subtract).then_inc(hid_lo_ready, 1)

            def split_x1(u):
                b, lo, hi = TAIL[u]
                dve.wait_ge(x1_hi_ready, u + 1)
                nc.vector.tensor_tensor(x1_lo[:, b, lo:hi], acc_ps[b][:, lo:hi], f32(x1_hi[:, b, lo:hi]),
                                        ALU.subtract).then_inc(x1_lo_ready, 1)

            def tail_hid(u, c):
                b, lo, hi = TAIL[u]
                dve.wait_ge(gate3_ready, HC * u + c + 1)
                dve.wait_ge(silu_ready, HC * u + c + 1)
                if u == 0:
                    dve.wait_ge(ug_bias_ready, 1)
                nc.vector.scalar_tensor_tensor(hid3[:, c, lo:hi], tail_banks(u, c)[1][:, lo:hi],
                                               ug_bias[:, b, HC + c:HC + c + 1], silu[:, c, lo:hi],
                                               ALU.add, ALU.mult).then_inc(hid3_ready, 1)

            def tail_hid_lo(u, c):
                b, lo, hi = TAIL[u]
                dve.wait_ge(hid3_hi_ready, HC * u + c + 1)
                nc.vector.tensor_tensor(hid3_lo[:, c, lo:hi], hid3[:, c, lo:hi], f32(hid3_hi[:, c, lo:hi]),
                                        ALU.subtract).then_inc(hid3_lo_ready, 1)

            def tail_result(u):
                b, lo, hi = TAIL[u]
                dve.wait_ge(out_ready, u + 1)
                if u == 0:
                    dve.wait_ge(out_bias_ready, 1)
                tiles = (hi - lo) // P
                nc.vector.tensor_tensor(result[:, b, lo:hi].rearrange("p (j d) -> p j d", d=D),
                                        tail_banks(u, 0)[2][:, lo:hi].rearrange("p (j d) -> p j d", d=D),
                                        out_bias[:, b, :].unsqueeze(1).to_broadcast([P, tiles, D]),
                                        ALU.add).then_inc(result_ready, 1)

            for n in range(STEPS):
                s, b, c = step_parts(n)
                dve.wait_ge(gelu_ready, n + 1)
                dve.wait_ge(up_ready, n + 1)
                if s == 0:
                    op = nc.vector.tensor_tensor(hid[:, n % RING, :], up_ps[n % 2][:, :], gelu[:, n % 2, :], ALU.mult)
                else:
                    k = (s - 1) % TOP
                    op = nc.vector.scalar_tensor_tensor(hid[:, n % RING, :], up_ps[n % 2][:, :], w_route[:, b, k:k + 1],
                                                        gelu[:, n % 2, :], ALU.mult, ALU.mult)
                op.then_inc(hid_ready, 1)
                if n == 0:
                    split_shared(DOWN)
                prepare(n)
                hid_low(n)
                if n == 17:
                    split_x1(0)
                if n in (18, 19):
                    tail_hid(0, n - 18)
                if n in (19, 20):
                    tail_hid_lo(0, n - 19)
                if n == 21:
                    tail_result(0)
            for u in (1,):
                split_x1(u)
            for u in (1,):
                for c in range(HC):
                    tail_hid(u, c)
                for c in range(HC):
                    tail_hid_lo(u, c)
            for u in (1,):
                tail_result(u)

        @block.tensor
        def _(pe):
            def product(dst, w_pair, v_pair, start, stop):
                nc.tensor.matmul(dst, w_pair[0], v_pair[0], start=start, stop=False)
                nc.tensor.matmul(dst, w_pair[1], v_pair[0], start=False, stop=False)
                return nc.tensor.matmul(dst, w_pair[0], v_pair[1], start=False, stop=stop)

            def turn_x(b):
                pe.wait_ge(x_in[b], 16)
                for j in range(J):
                    last = nc.tensor.transpose(work_ps[b][:, j * P:(j + 1) * P], x_tok[:, b, j * P:(j + 1) * P], ident[:, :])
                last.then_inc(xT_ready, 1)

            def residual(b):
                pe.wait_ge(xT_hi_ready, b + 1)
                nc.tensor.matmul(acc_ps[b][:, :], ident_r[:, :], xT_hi[:, b, :], start=True, stop=False)
                pe.wait_ge(xT_lo_ready, b + 1)
                nc.tensor.matmul(acc_ps[b][:, :], ident_r[:, :], xT_lo[:, b, :], start=False, stop=False)

            def hidden(n):
                s, b, c = step_parts(n)
                xT = (xT_hi[:, b, :], xT_lo[:, b, :])
                cols = slice(c * P, (c + 1) * P)
                if c == 0:
                    pe.wait_ge(w_hi_ready[s], GATE + 1)
                    pe.wait_ge(w_lo_ready[s], GATE + 1)
                if n >= 2:
                    pe.wait_ge(gelu_ready, n - 1)
                product(gate_ps[n % 2][:, :], (w_hi[:, s, GATE, cols], w_lo[:, s, GATE, cols]), xT,
                        True, True).then_inc(gate_ready, 1)
                if c == 0:
                    pe.wait_ge(w_hi_ready[s], UP + 1)
                    pe.wait_ge(w_lo_ready[s], UP + 1)
                if n >= 2:
                    pe.wait_ge(hid_ready, n - 1)
                product(up_ps[n % 2][:, :], (w_hi[:, s, UP, cols], w_lo[:, s, UP, cols]), xT,
                        True, True).then_inc(up_ready, 1)

            def down(n, lo=0, hi=S):
                s, b, c = step_parts(n)
                cols = slice(c * P, (c + 1) * P)
                if c == 0:
                    pe.wait_ge(w_hi_ready[s], DOWN + 1)
                    pe.wait_ge(w_lo_ready[s], DOWN + 1)
                closes = n + 1 in (FIRST_STEPS, STEPS)
                w = (w_hi[:, s, DOWN, cols], w_lo[:, s, DOWN, cols])
                dst = acc_ps[b][:, lo:hi]
                pe.wait_ge(hid_hi_ready, n + 1)
                nc.tensor.matmul(dst, w[0], hid_hi[:, n % RING, lo:hi], start=False, stop=False)
                nc.tensor.matmul(dst, w[1], hid_hi[:, n % RING, lo:hi], start=False, stop=False)
                pe.wait_ge(hid_lo_ready, n + 1)
                return nc.tensor.matmul(dst, w[0], hid_lo[:, n % RING, lo:hi], start=False, stop=closes)

            def prepare(n):
                if n == 5:
                    pe.wait_ge(l1_in, 16 * 4)
                    pe.wait_ge(xT_lo_ready, B)
                    pe.wait_ge(bs_mix_ready, B)
                    for b in range(B):
                        nc.tensor.transpose(work_ps[0][:, b * P:(b + 1) * P],
                                            bs_mix[:, b, :, :].rearrange("o e r -> o (e r)"), ident[:, :])
                    pe.wait_ge(masked_ready, 1)
                    for b in range(B):
                        last = nc.tensor.transpose(work_ps[0][:, (B + b) * P:(B + b + 1) * P], mix_masked[:, b, :], ident[:, :])
                    last.then_inc(prep_mm, 1)
                if n == 6:
                    pe.wait_ge(bsT_ready, 1)
                    for b in range(B):
                        last = nc.tensor.matmul(work_ps[1][:, b * P:(b + 1) * P], bsT[:, b, :], as_sb[:, :],
                                                start=True, stop=True)
                    last.then_inc(prep_mm, 1)
                if n == 7:
                    pe.wait_ge(A2_ready, 1)
                    pe.wait_ge(A1T_ready, 1)
                    for b in range(B):
                        nc.tensor.matmul(work_ps[0][:, b * P:(b + 1) * P], A2[:, b, :], A1T[:, b, :], start=True, stop=True)
                    for b in range(B):
                        last = nc.tensor.matmul(work_ps[0][:, (B + b) * P:(B + b + 1) * P], A1T[:, b, :], A2[:, b, :],
                                                start=True, stop=True)
                    last.then_inc(prep_mm, 1)
                if n == 8:
                    pe.wait_ge(b1_wide_ready, 1)
                    for b in range(B):
                        nc.tensor.matmul(work_ps[1][:, b:b + 1], A2[:, b, :], b1_col[:, 0:1], start=True, stop=True)
                    for b in range(B):
                        last = nc.tensor.matmul(work_ps[1][:, (1 + b) * P:(2 + b) * P], b1_wide[:, :], A2[:, b, :],
                                                start=True, stop=True)
                    last.then_inc(prep_mm, 1)
                if n in (9, 10):
                    b = n - 9
                    pe.wait_ge(l3_in[b], 16 * 7)
                    if b == 0:
                        pe.wait_ge(QT_ready, 1)
                        pe.wait_ge(Q_lo_ready, 1)
                    else:
                        pe.wait_ge(out_bias_ready, 1)
                    for k in range(2 * HC):
                        last = nc.tensor.transpose(work_ps[b][:, k * P:(k + 1) * P], upgate_raw[:, b, k, :], ident[:, :])
                    last.then_inc(prep_mm, 1)
                if n == 11:
                    pe.wait_ge(upgateT_ready, 1)
                    for b in range(B):
                        for c in range(HC):
                            k = b * HC + c
                            last = nc.tensor.transpose(work_ps[0][:, k * P:(k + 1) * P], down_raw[:, b, :, c], ident[:, :])
                    last.then_inc(prep_mm, 1)
                if n in (12, 13):
                    b = n - 12
                    pe.wait_ge(upgateT_ready, B)
                    if b == 1:
                        pe.wait_ge(downT_lo_ready, 1)
                    nc.tensor.matmul(work_ps[1 - b][:, :], QT[:, b, :], upgateT[:, b, :], start=True,
                                     stop=True).then_inc(prep_mm, 1)
                if n == 14:
                    pe.wait_ge(cb_ready, 1)
                    pe.wait_ge(R_lo_ready, 1)
                    for b in range(B):
                        for k in range(2 * HC):
                            col = b * 2 * HC + k
                            last = nc.tensor.matmul(work_ps[1][:, col:col + 1], upgateT[:, b, k * P:(k + 1) * P],
                                                    cb_col[:, b:b + 1], start=True, stop=True)
                    last.then_inc(prep_mm, 1)

            def tail_up_gate(u, c):
                b, lo, hi = TAIL[u]
                up, gate, _ = tail_banks(u, c)
                x1 = (x1_hi[:, b, lo:hi], x1_lo[:, b, lo:hi])
                if c == 0:
                    pe.wait_ge(x1_hi_ready, u + 1)
                    pe.wait_ge(x1_lo_ready, u + 1)
                if u == 0 and c == 0:
                    pe.wait_ge(R_lo_ready, B)
                    pe.wait_ge(ug_bias_ready, 1)
                if u == 0 and c == 1:
                    pe.wait_ge(hid3_ready, 1)
                if u == 1:
                    pe.wait_ge(gelu_ready, STEPS)
                    pe.wait_ge(hid_ready, STEPS)
                for dst, k, done in ((up, c, up3_ready), (gate, HC + c, gate3_ready)):
                    cols = slice(k * P, (k + 1) * P)
                    product(dst[:, lo:hi], (R_hi[:, b, cols], R_lo[:, b, cols]), x1, True, True).then_inc(done, 1)

            def tail_residual(u):
                b, lo, hi = TAIL[u]
                dst = tail_banks(u, 0)[2]
                if u == 0:
                    pe.wait_ge(Q_lo_ready, 1)
                if u == 1:
                    pe.wait_ge(hid3_ready, HC)
                for t in range(lo, hi, P):
                    product(dst[:, t:t + P], (x1_hi[:, b, t:t + P], x1_lo[:, b, t:t + P]),
                            (Q_hi[:, b, :], Q_lo[:, b, :]), t == lo, False)

            def tail_down(u, c):
                b, lo, hi = TAIL[u]
                dst = tail_banks(u, 0)[2]
                pe.wait_ge(hid3_hi_ready, HC * u + c + 1)
                pe.wait_ge(hid3_lo_ready, HC * u + c + 1)
                if u == 0:
                    pe.wait_ge(downT_lo_ready, 1)
                for t in range(lo, hi, P):
                    last = product(dst[:, t:t + P], (hid3_hi[:, c, t:t + P], hid3_lo[:, c, t:t + P]),
                                   (downT_hi[:, b, c, :], downT_lo[:, b, c, :]), False, c == HC - 1 and t + P == hi)
                if c == HC - 1:
                    last.then_inc(out_ready, 1)

            pe.wait_ge(ident_ready, 1)
            turn_x(0)
            turn_x(1)
            pe.wait_ge(ident_ready, 2)
            residual(0)
            for n in range(STEPS):
                hidden(n)
                if n == 0:
                    residual(1)
                if n >= LAG:
                    down(n - LAG).then_inc(down_done, 1)
                prepare(n)
                if n == 18:
                    tail_up_gate(0, 0)
                if n == 19:
                    tail_residual(0)
                    tail_up_gate(0, 1)
                if n in (20, 21):
                    tail_down(0, n - 20)
            for u in (1,):
                _, lo, hi = TAIL[u]
                down(STEPS - 2, lo, hi)
                down(STEPS - 1, lo, hi).then_inc(acc_ready, 1)
            for u in (1,):
                for c in range(HC):
                    tail_up_gate(u, c)
                tail_residual(u)
            for u in (1,):
                for c in range(HC):
                    tail_down(u, c)


_INS = ['x', 'cond_8', 'L0_cond_skill_gate', 'L0_cond_skill_up', 'L0_cond_skill_down', 'L0_cond_shared_gate',
        'L0_cond_shared_up', 'L0_cond_shared_down', 'L1_cond_W_base', 'L1_cond_b_base', 'L1_cond_As', 'L1_cond_Bs',
        'L2_cond_weight', 'L2_cond_mask', 'L2_cond_bias', 'L3_cond_W_up', 'L3_cond_b_up', 'L3_cond_W_gate',
        'L3_cond_b_gate', 'L3_cond_W_down', 'L3_cond_b_down']


def kernel(**inputs):
    import numpy as _np
    import concourse.bacc as _bacc
    from concourse import mybir as _mybir
    from concourse.bass_utils import run_bass_kernel_spmd as _run

    nc = _bacc.Bacc("TRN2", target_bir_lowering=False, num_devices=1)
    arrays, args = {}, []
    for name in _INS:
        a = _np.ascontiguousarray(inputs[name])
        arrays[f"in_{name}_dram"] = a
        args.append(nc.dram_tensor(f"in_{name}_dram", a.shape, _mybir.dt.from_np(a.dtype), kind="ExternalInput").ap())
    out = nc.dram_tensor("out_0_dram", inputs["x"].shape, _mybir.dt.from_np(_np.dtype("float32")), kind="ExternalOutput").ap()
    build(nc, *args, out)
    r = _run(nc, [arrays], core_ids=[0])
    return r.results[0]["out_0_dram"]
```

```python
import concourse.bass as bass
from concourse import mybir
from contextlib import ExitStack


def build(nc, x, cond, sk_gate, sk_up, sk_down, sh_gate, sh_up, sh_down, W_base, b_base, As, Bs,
          weight, mask, bias, W_up, b_up, W_gate, b_gate, W_down, b_down, out):
    F32, F32R, U32 = mybir.dt.float32, mybir.dt.float32r, mybir.dt.uint32
    ALU, ACT, AX = mybir.AluOpType, mybir.ActivationFunctionType, mybir.AxisListType

    B, S, D = x.shape
    E, _, I = sk_gate.shape
    R = As.shape[1]
    H = W_up.shape[1]
    P = 128
    J = S // P
    C = I // P
    HC = H // P
    TOP = 2
    LORA_SCALE = 32.0 / R
    ROUTE_SCALE = 1.0 / 12
    assert D == P and E * R == P and E == 8

    BLOCKS = [(0, 0), (0, 1)] + [(1 + TOP * b + k, b) for b in range(B) for k in range(TOP)]
    SETS = 1 + TOP * B
    STEPS = len(BLOCKS) * C
    FIRST_STEPS = (B + TOP) * C
    LAG = 2
    GATE, UP, DOWN = range(3)
    RING = 3

    WARM_BEFORE_X, WARM_AFTER_X = 4, 2
    EXP_STEP = 1
    ROUTE_STEPS = 5
    FOLDS = [P >> k for k in range(1, P.bit_length())]
    MIX = 3
    PREP = MIX + E + 1
    DVE_HI = (1, 2, STEPS - 1)
    PAIR = 2
    OUT_PARTS = B * J // PAIR
    X1_STEP = FIRST_STEPS - 1 + LAG

    ctx = ExitStack()
    with ctx:
        def sb(name, shape, dt=F32):
            return ctx.enter_context(nc.sbuf_tensor(name, shape, dt))

        def ps(name):
            return ctx.enter_context(nc.psum_tensor(name, [P, 512], F32))

        def sem(name):
            return ctx.enter_context(nc.semaphore(name))

        ident = sb("ident", [P, P])
        ident_r = sb("ident_r", [P, P], F32R)
        cond_all = sb("cond_all", [P, B, E])
        top_val = sb("top_val", [P, B, 8])
        top_idx = sb("top_idx", [P, B, 8], U32)
        neg_max = sb("neg_max", [P, B])
        top_exp = sb("top_exp", [P, B, TOP])
        exp_sum = sb("exp_sum", [P, B, 1])
        exp_inv = sb("exp_inv", [P, B, 1])
        w_norm = sb("w_norm", [P, B, TOP])
        w_stop = sb("w_stop", [P, B, TOP])
        w_route = sb("w_route", [P, B, TOP])
        x_tok = sb("x_tok", [P, B, S])
        xT_hi = sb("xT_hi", [P, B, S], F32R)
        xT_lo = sb("xT_lo", [P, B, S], F32R)
        w_raw = sb("w_raw", [P, SETS, 3, I])
        w_hi = sb("w_hi", [P, SETS, 3, I], F32R)
        w_lo = sb("w_lo", [P, SETS, 3, I], F32R)
        gelu = sb("gelu", [P, 2, S])
        hid = sb("hid", [P, RING, S])
        hid_hi = sb("hid_hi", [P, RING, S], F32R)
        hid_lo = sb("hid_lo", [P, RING, S], F32R)
        base_sb = sb("base_sb", [P, P])
        base_id = sb("base_id", [P, P])
        b1_col = sb("b1_col", [P, 1])
        b1_wide = sb("b1_wide", [P, P])
        as_sb = sb("as_sb", [P, P])
        bs_sb = sb("bs_sb", [P, E, R])
        bs_mix = sb("bs_mix", [P, B, E, R])
        bsT = sb("bsT", [P, B, P])
        mix_w = sb("mix_w", [P, E, P])
        mask_sb = sb("mask_sb", [P, P])
        mix_acc = sb("mix_acc", [P, B, P])
        mix_masked = sb("mix_masked", [P, B, P])
        A1T = sb("A1T", [P, B, P])
        A2 = sb("A2", [P, B, P])
        QT = sb("QT", [P, B, P])
        Q_sp = sb("Q_sp", [P, B, 2, P], F32R)
        cb_row = sb("cb_row", [P, B, P])
        upgate_raw = sb("upgate_raw", [P, B, 2 * HC, P])
        down_raw = sb("down_raw", [P, B, P, HC])
        bug_col = sb("bug_col", [P, B, 2, HC])
        row_bias = sb("row_bias", [P, B, 2, P])
        bias_prod = sb("bias_prod", [P, B, 2 * HC, P])
        out_bias = sb("out_bias", [P, B, P])
        upgateT = sb("upgateT", [P, B, 2 * HC * P])
        downT_sp = sb("downT_sp", [P, B, HC, 2, P], F32R)
        R_hi = sb("R_hi", [P, B, 2 * HC * P], F32R)
        R_lo = sb("R_lo", [P, B, 2 * HC * P], F32R)
        ug_bias = sb("ug_bias", [P, B, 2 * HC])
        x1_hi = sb("x1_hi", [P, B, S], F32R)
        x1_lo = sb("x1_lo", [P, B, S], F32R)
        silu = sb("silu", [P, HC, S])
        hid3 = sb("hid3", [P, HC, S])
        hid3_hi = sb("hid3_hi", [P, B, HC, S], F32R)
        hid3_lo = sb("hid3_lo", [P, B, HC, S], F32R)
        corr = sb("corr", [P, OUT_PARTS, PAIR, D])
        result = gelu
        table_scratch = sb("table_scratch", [P, 2])

        gate_ps = [ps("gate_ps0"), ps("gate_ps1")]
        up_ps = [ps("up_ps0"), ps("up_ps1")]
        acc_ps = [ps("acc_ps0"), ps("acc_ps1")]
        work_ps = [ps("work_ps0"), ps("work_ps1")]

        cond_in = sem("cond_in")
        x_in = [sem(f"x_in{b}") for b in range(B)]
        w_in = [[sem(f"w_in{s}_{m}") for m in range(3)] for s in range(SETS)]
        l1_in, l2_in = sem("l1_in"), sem("l2_in")
        l3_in = [sem(f"l3_in{b}") for b in range(B)]
        stored = [sem(f"stored{k}") for k in range(OUT_PARTS)]
        ident_set, ident_ready = sem("ident_set"), sem("ident_ready")
        bs_mix_ready = sem("bs_mix_ready")
        base_ready, b1_wide_ready = sem("base_ready"), sem("b1_wide_ready")
        top_found, neg_max_ready, top_exp_ready = sem("top_found"), sem("neg_max_ready"), sem("top_exp_ready")
        route_step = sem("route_step")
        scratch_ready, tables_loaded = sem("scratch_ready"), sem("tables_loaded")
        xT_ready, xT_hi_ready, xT_lo_ready = sem("xT_ready"), sem("xT_hi_ready"), sem("xT_lo_ready")
        w_hi_ready = [[sem(f"w_hi_ready{s}_{m}") for m in range(3)] for s in range(SETS)]
        w_lo_ready = [[sem(f"w_lo_ready{s}_{m}") for m in range(3)] for s in range(SETS)]
        gate_ready, up_ready, down_done = sem("gate_ready"), sem("up_ready"), sem("down_done")
        gelu_ready, hid_ready = sem("gelu_ready"), sem("hid_ready")
        hid_hi_ready, hid_lo_ready = sem("hid_hi_ready"), sem("hid_lo_ready")
        mix_step, masked_ready = sem("mix_step"), sem("masked_ready")
        prep_mm = sem("prep_mm")
        bsT_ready, A2_ready, A1T_ready = sem("bsT_ready"), sem("A2_ready"), sem("A1T_ready")
        QT_ready, Q_hi_ready, Q_lo_ready = sem("QT_ready"), sem("Q_hi_ready"), sem("Q_lo_ready")
        cb_row_ready, out_bias_ready = sem("cb_row_ready"), sem("out_bias_ready")
        bias_fold = [sem(f"bias_fold{b}") for b in range(B)]
        upgateT_ready = sem("upgateT_ready")
        downT_hi_ready, downT_lo_ready = sem("downT_hi_ready"), sem("downT_lo_ready")
        R_hi_ready, R_lo_ready = sem("R_hi_ready"), sem("R_lo_ready")
        ug_bias_ready = sem("ug_bias_ready")
        x1_hi_ready, x1_lo_ready = sem("x1_hi_ready"), sem("x1_lo_ready")
        up3_ready, gate3_ready = sem("up3_ready"), sem("gate3_ready")
        silu_ready, hid3_ready = sem("silu_ready"), sem("hid3_ready")
        hid3_hi_ready, hid3_lo_ready = sem("hid3_hi_ready"), sem("hid3_lo_ready")
        out_ready, corr_ready, result_ready = sem("out_ready"), sem("corr_ready"), sem("result_ready")

        (ST_BS, ST_A, ST_Q, ST_BIAS, ST_UGT0, ST_UGT1, ST_DNT, ST_R0, ST_R1) = range(9)

        def f32(ap):
            return ap.bitcast(F32)

        def step_parts(n):
            s, b = BLOCKS[n // C]
            return s, b, n % C

        def tail_banks(u, c):
            return {(0, 0): work_ps, (0, 1): (up_ps[0], gate_ps[0]),
                    (1, 0): (acc_ps[1], gate_ps[1]), (1, 1): work_ps}[u, c]

        def out_bank(u, k):
            return ((acc_ps[0], up_ps[1]), (up_ps[0], gate_ps[0]))[u][k][:, :].rearrange("p (j m d) -> p j m d", j=PAIR, m=2)

        block = ctx.enter_context(nc.Block())

        @block.sync
        def _(sp):
            def load_x(b):
                sp.dma_start(x_tok[:, b, :], x[b, :, :].rearrange("(p j) d -> p (j d)", j=J)).then_inc(x_in[b], 16)

            load_x(0)
            sp.dma_start(w_raw[:, 0, GATE, :], sh_gate).then_inc(w_in[0][GATE], 16)
            sp.dma_start(cond_all[:, :, :], cond.rearrange("b e -> (b e)").partition_broadcast(P)).then_inc(cond_in, 16)
            sp.dma_start(w_raw[:, 0, UP, :], sh_up).then_inc(w_in[0][UP], 16)
            load_x(1)
            sp.dma_start(w_raw[:, 0, DOWN, :].rearrange("p (c h) -> p c h", c=C),
                         sh_down.rearrange("(c p) h -> p c h", p=P)).then_inc(w_in[0][DOWN], 16)

            def load_expert(s, e):
                one = bass.ds(e, 1)
                for m, w in ((GATE, sk_gate), (UP, sk_up)):
                    sp.dma_start(w_raw[:, s, m, :], w[one, :, :].rearrange("e h i -> h (e i)")).then_inc(w_in[s][m], 16)
                sp.dma_start(w_raw[:, s, DOWN, :].rearrange("p (c h) -> p c h", c=C),
                             sk_down[one, :, :].rearrange("e (c p) h -> p (e c) h", p=P)).then_inc(w_in[s][DOWN], 16)

            def load_l3(b, e):
                one = bass.ds(e, 1)
                for m, w in ((0, W_up), (1, W_gate)):
                    sp.dma_start(upgate_raw[:, b, m * HC:(m + 1) * HC, :],
                                 w[one, :, :].rearrange("e (p c) d -> p (e c) d", c=HC)).then_inc(l3_in[b], 16)
                sp.dma_start(down_raw[:, b, :, :],
                             W_down[one, :, :].rearrange("e d (p c) -> d (e p) c", c=HC)).then_inc(l3_in[b], 16)
                for m, v in ((0, b_up), (1, b_gate)):
                    sp.dma_start(bug_col[:, b, m, :],
                                 v[one, :].rearrange("e (p c) -> p (e c)", c=HC)).then_inc(l3_in[b], 16)
                sp.dma_start(row_bias[:, b, 1, :],
                             b_down[one, :].rearrange("e d -> (e d)").partition_broadcast(P)).then_inc(l3_in[b], 16)

            sp.wait_ge(top_found, B)
            first = [sp.value_load(top_idx[0:1, b, 0:1], min_val=0, max_val=E - 1) for b in range(B)]
            second = [sp.value_load(top_idx[0:1, b, 1:2], min_val=0, max_val=E - 1) for b in range(B)]
            load_expert(1, first[0])
            with nc.allow_non_contiguous_dma(reason="128 single values"):
                sp.dma_start(b1_col[:, :], b_base.rearrange("(o a) -> o a", a=1)).then_inc(l1_in, 16)
            sp.dma_start(as_sb[:, :], As.rearrange("e r c -> (e r) c")).then_inc(l1_in, 16)
            sp.dma_start(bs_sb[:, :, :], Bs.rearrange("e o r -> o e r")).then_inc(l1_in, 16)
            sp.dma_start(base_sb[:, :], W_base).then_inc(l1_in, 16)
            sp.dma_start(mix_w[:, :, :], weight.rearrange("g o t -> o g t")).then_inc(l2_in, 16)
            sp.dma_start(mask_sb[:, :], mask).then_inc(l2_in, 16)
            load_expert(2, second[0])
            for b in range(B):
                sp.dma_start(row_bias[:, b, 0, :], bias.partition_broadcast(P)).then_inc(l3_in[b], 16)
                load_l3(b, first[b])
            load_expert(3, first[1])
            load_expert(4, second[1])
            for k in range(OUT_PARTS):
                u, lo = k // PAIR, k % PAIR * PAIR * D
                sp.wait_ge(result_ready, k + 1)
                sp.dma_start(out[u, :, :].rearrange("(p j) d -> p (j d)", j=J)[:, lo:lo + PAIR * D],
                             result[:, u, lo:lo + PAIR * D]).then_inc(stored[k], 16)
            for k in range(OUT_PARTS):
                sp.wait_ge(stored[k], 16)

        @block.gpsimd
        def _(pool):
            nc.gpsimd.memset(ident[:, :], 0.0).then_inc(ident_set, 1)
            pool.wait_ge(ident_set, 1)
            nc.gpsimd.affine_select(out=ident[:, :], in_=ident[:, :], compare_op=ALU.not_equal, fill=1.0, base=0,
                                    pattern=[[-1, P]], channel_multiplier=1).then_inc(ident_ready, 1)
            pool.wait_ge(ident_ready, 1)
            nc.gpsimd.tensor_copy(ident_r[:, :], ident[:, :]).then_inc(ident_ready, 1)

            def split_weight(s, m):
                pool.wait_ge(w_hi_ready[s][m], 1)
                nc.gpsimd.tensor_tensor(w_lo[:, s, m, :], w_raw[:, s, m, :], f32(w_hi[:, s, m, :]),
                                        ALU.subtract).then_inc(w_lo_ready[s][m], 1)

            for m in range(3):
                split_weight(1, m)
            pool.wait_ge(l1_in, 16 * 4)
            pool.wait_ge(cond_in, 16)
            for b in range(B):
                nc.gpsimd.tensor_tensor(bs_mix[:, b, :, :], bs_sb[:, :, :],
                                        cond_all[:, b, :].unsqueeze(2).to_broadcast([P, E, R]),
                                        ALU.mult).then_inc(bs_mix_ready, 1)
            nc.gpsimd.tensor_tensor(base_id[:, :], base_sb[:, :], ident[:, :], ALU.add).then_inc(base_ready, 1)
            nc.gpsimd.tensor_copy(b1_wide[:, :], b1_col[:, 0:1].to_broadcast([P, P])).then_inc(b1_wide_ready, 1)
            for m in range(3):
                split_weight(2, m)
            for s in range(3, SETS):
                for m in range(3):
                    split_weight(s, m)
            pool.wait_ge(cb_row_ready, 1)
            for b in range(B):
                pool.wait_ge(l3_in[b], 16 * 7)
                nc.gpsimd.tensor_tensor(bias_prod[:, b, :, :], upgate_raw[:, b, :, :],
                                        cb_row[:, b, :].unsqueeze(1).to_broadcast([P, 2 * HC, P]),
                                        ALU.mult).then_inc(bias_fold[b], 1)
                nc.gpsimd.tensor_tensor(out_bias[:, b, :], cb_row[:, b, :], row_bias[:, b, 1, :],
                                        ALU.add).then_inc(out_bias_ready, 1)
            for fold, half in enumerate(FOLDS):
                for b in range(B):
                    pool.wait_ge(bias_fold[b], fold + 1)
                    nc.gpsimd.tensor_tensor(bias_prod[:, b, :, 0:half], bias_prod[:, b, :, 0:half],
                                            bias_prod[:, b, :, half:2 * half], ALU.add).then_inc(bias_fold[b], 1)
            for b in range(B):
                pool.wait_ge(bias_fold[b], len(FOLDS) + 1)
                nc.gpsimd.tensor_tensor(ug_bias[:, b, :], bias_prod[:, b, :, 0], bug_col[:, b, :, :].rearrange("p m c -> p (m c)"),
                                        ALU.add).then_inc(ug_bias_ready, 1)
            pool.wait_ge(hid3_hi_ready, HC + 1)
            nc.gpsimd.tensor_tensor(hid3_lo[:, 1, 0, :], hid3[:, 0, :], f32(hid3_hi[:, 1, 0, :]),
                                    ALU.subtract).then_inc(hid3_lo_ready, 1)

        @block.scalar
        def _(act):
            def route_exp():
                act.wait_ge(neg_max_ready, 1)
                for b in range(B):
                    nc.scalar.activation(top_exp[:, b, :], top_val[:, b, 0:TOP], ACT.Exp,
                                         bias=neg_max[:, b:b + 1]).then_inc(top_exp_ready, 1)

            def split_x(b):
                act.wait_ge(xT_ready, b + 1)
                nc.scalar.activation(xT_hi[:, b, :], work_ps[b][:, :], ACT.Copy).then_inc(xT_hi_ready, 1)

            def split_weight(s, m):
                act.wait_ge(w_in[s][m], 16)
                nc.scalar.activation(w_hi[:, s, m, :], w_raw[:, s, m, :], ACT.Copy).then_inc(w_hi_ready[s][m], 1)

            act.wait_ge(scratch_ready, 1)
            nc.scalar.activation(table_scratch[:, 1:2], table_scratch[:, 0:1], ACT.Gelu_apprx_tanh).then_inc(tables_loaded, 1)
            split_x(0)
            split_weight(0, UP)

            def prepare(n):
                if n == EXP_STEP:
                    route_exp()
                k = n - EXP_STEP - 2
                if 0 <= k < 3 * (SETS - 1):
                    split_weight(1 + k // 3, k % 3)
                if n == PREP + ST_BS:
                    act.wait_ge(prep_mm, ST_BS + 1)
                    nc.scalar.activation(bsT[:, :, :], work_ps[0][:, 0:B * P], ACT.Copy, scale=LORA_SCALE).then_inc(bsT_ready, 1)

            def leave_work_banks(n):
                if n == PREP + ST_Q:
                    act.wait_ge(prep_mm, ST_Q + 1)
                    nc.scalar.activation(QT[:, :, :], work_ps[0][:, 0:B * P], ACT.Copy).then_inc(QT_ready, 1)
                    nc.scalar.activation(Q_sp[:, :, 0, :], work_ps[0][:, B * P:2 * B * P].rearrange("p (b d) -> p b d", b=B),
                                         ACT.Copy).then_inc(Q_hi_ready, 1)
                for b in range(B):
                    if n == PREP + ST_UGT0 + b:
                        act.wait_ge(prep_mm, ST_UGT0 + b + 1)
                        nc.scalar.activation(upgateT[:, b, :], work_ps[b][:, :], ACT.Copy).then_inc(upgateT_ready, 1)
                if n == PREP + ST_DNT:
                    act.wait_ge(prep_mm, ST_DNT + 1)
                    nc.scalar.activation(downT_sp[:, :, :, 0, :], work_ps[0][:, :].rearrange("p (b c d) -> p b c d", b=B, c=HC),
                                         ACT.Copy).then_inc(downT_hi_ready, 1)
                for b in range(B):
                    if n == PREP + ST_R0 + b:
                        act.wait_ge(prep_mm, ST_R0 + b + 1)
                        nc.scalar.activation(R_hi[:, b, :], work_ps[1 - b][:, :], ACT.Copy).then_inc(R_hi_ready, 1)

            def split_x1(u):
                if u == 0:
                    act.wait_ge(down_done, FIRST_STEPS)
                else:
                    act.wait_ge(down_done, STEPS)
                nc.scalar.activation(x1_hi[:, u, :], acc_ps[u][:, :], ACT.Copy).then_inc(x1_hi_ready, 1)

            def tail_silu(u, c):
                act.wait_ge(up3_ready, HC * u + c + 1)
                if (u, c) == (0, 0):
                    act.wait_ge(ug_bias_ready, B)
                if u:
                    act.wait_ge(hid3_ready, c + 1)
                nc.scalar.activation(silu[:, c, :], tail_banks(u, c)[0][:, :], ACT.Silu,
                                     bias=ug_bias[:, u, c:c + 1]).then_inc(silu_ready, 1)

            def tail_hid_hi(u, c):
                act.wait_ge(hid3_ready, HC * u + c + 1)
                nc.scalar.activation(hid3_hi[:, u, c, :], hid3[:, c, :], ACT.Copy).then_inc(hid3_hi_ready, 1)

            def gelu_gate(n):
                act.wait_ge(gate_ready, n + 1)
                if n >= 2:
                    act.wait_ge(hid_ready, n - 1)
                nc.scalar.activation(gelu[:, n % 2, :], gate_ps[n % 2][:, :], ACT.Gelu_apprx_tanh).then_inc(gelu_ready, 1)

            def hid_high(n):
                act.wait_ge(hid_ready, n + 1)
                if n >= RING:
                    act.wait_ge(down_done, n - RING + 1)
                nc.scalar.activation(hid_hi[:, n % RING, :], hid[:, n % RING, :], ACT.Copy).then_inc(hid_hi_ready, 1)

            for n in range(STEPS):
                if n < STEPS - 1:
                    gelu_gate(n)
                if n == 0:
                    split_weight(0, DOWN)
                    split_x(1)
                prepare(n)
                if n == STEPS - 2:
                    gelu_gate(STEPS - 1)
                if n not in DVE_HI:
                    hid_high(n)
                leave_work_banks(n)
                if n == X1_STEP:
                    split_x1(0)
            act.wait_ge(ug_bias_ready, B)
            nc.scalar.activation(table_scratch[:, 1:2], ug_bias[:, 0, 0:1], ACT.Silu).then_inc(tables_loaded, 1)
            tail_silu(0, 0)
            split_x1(1)
            tail_silu(0, 1)
            tail_hid_hi(0, 1)
            tail_silu(1, 0)
            tail_silu(1, 1)
            tail_hid_hi(1, 1)

        @block.vector
        def _(dve):
            nc.vector.memset(table_scratch[:, 0:1], 0.0).then_inc(scratch_ready, 1)
            def route_weights(step):
                if step == 0:
                    dve.wait_ge(top_exp_ready, B)
                    op = nc.vector.tensor_tensor(exp_sum[:, :, :], top_exp[:, :, 0:1], top_exp[:, :, 1:2], ALU.add)
                else:
                    dve.wait_ge(route_step, B + step)
                if step == 1:
                    op = nc.vector.reciprocal(exp_inv[:, :, :], exp_sum[:, :, :])
                if step == 2:
                    op = nc.vector.tensor_tensor(w_norm[:, :, :], top_exp[:, :, :], exp_inv[:, :, :].to_broadcast([P, B, TOP]), ALU.mult)
                if step == 3:
                    op = nc.vector.tensor_scalar(w_stop[:, :, :], w_norm[:, :, :], 1.0 - ROUTE_SCALE, None, ALU.mult)
                if step == 4:
                    op = nc.vector.scalar_tensor_tensor(w_route[:, :, :], w_norm[:, :, :], ROUTE_SCALE, w_stop[:, :, :],
                                                        ALU.mult, ALU.add)
                op.then_inc(route_step, 1)

            def split_x(b):
                dve.wait_ge(xT_hi_ready, b + 1)
                nc.vector.tensor_tensor(xT_lo[:, b, :], work_ps[b][:, :], f32(xT_hi[:, b, :]),
                                        ALU.subtract).then_inc(xT_lo_ready, 1)

            def split_shared(m, lo, hi):
                dve.wait_ge(w_hi_ready[0][m], 1 if lo == 0 or m != GATE else 2)
                nc.vector.tensor_tensor(w_lo[:, 0, m, lo:hi], w_raw[:, 0, m, lo:hi], f32(w_hi[:, 0, m, lo:hi]),
                                        ALU.subtract).then_inc(w_lo_ready[0][m], 1)

            dve.wait_ge(w_in[0][GATE], 16)
            nc.vector.tensor_copy(w_hi[:, 0, GATE, 0:P], w_raw[:, 0, GATE, 0:P]).then_inc(w_hi_ready[0][GATE], 1)
            split_shared(GATE, 0, P)
            dve.wait_ge(cond_in, 16)
            for b in range(B):
                nc.vector.max(top_val[:, b, :], cond_all[:, b, :]).then_inc(route_step, 1)
            dve.wait_ge(route_step, B)
            for b in range(B):
                nc.vector.max_index(top_idx[:, b, :], top_val[:, b, :], cond_all[:, b, :]).then_inc(top_found, 1)
            nc.vector.tensor_scalar(neg_max[:, :], top_val[:, :, 0], -1.0, None, ALU.mult).then_inc(neg_max_ready, 1)
            nc.vector.tensor_copy(w_hi[:, 0, GATE, P:I], w_raw[:, 0, GATE, P:I]).then_inc(w_hi_ready[0][GATE], 1)
            split_x(0)
            split_shared(UP, 0, P)
            split_shared(GATE, P, I)
            split_shared(UP, P, I)

            def mix(g):
                for b in range(B):
                    y = cond_all[:, b, g:g + 1]
                    if g == 0:
                        dve.wait_ge(l2_in, 16 * 2)
                        op = nc.vector.tensor_scalar(mix_acc[:, b, :], mix_w[:, g, :], y, None, ALU.mult)
                    else:
                        dve.wait_ge(mix_step, B * (g - 1) + b + 1)
                        op = nc.vector.scalar_tensor_tensor(mix_acc[:, b, :], mix_w[:, g, :], y, mix_acc[:, b, :],
                                                            ALU.mult, ALU.add)
                    op.then_inc(mix_step, 1)

            def prepare(n):
                if 0 <= n - EXP_STEP - 1 < ROUTE_STEPS:
                    route_weights(n - EXP_STEP - 1)
                if MIX <= n < MIX + E:
                    mix(n - MIX)
                if n == MIX + E:
                    dve.wait_ge(mix_step, B * E)
                    nc.vector.tensor_tensor(mix_masked[:, :, :], mix_acc[:, :, :],
                                            mask_sb[:, :].unsqueeze(1).to_broadcast([P, B, P]),
                                            ALU.mult).then_inc(masked_ready, 1)

            def leave_work_banks(n):
                if n == PREP + ST_A:
                    dve.wait_ge(prep_mm, ST_A + 1)
                    nc.vector.tensor_tensor(A2[:, :, :], work_ps[0][:, B * P:2 * B * P].rearrange("p (b o) -> p b o", b=B),
                                            ident[:, :].unsqueeze(1).to_broadcast([P, B, P]),
                                            ALU.add).then_inc(A2_ready, 1)
                    dve.wait_ge(base_ready, 1)
                    nc.vector.tensor_tensor(A1T[:, :, :], work_ps[1][:, 0:B * P].rearrange("p (b c) -> p b c", b=B),
                                            base_id[:, :].unsqueeze(1).to_broadcast([P, B, P]),
                                            ALU.add).then_inc(A1T_ready, 1)
                if n == PREP + ST_Q:
                    dve.wait_ge(Q_hi_ready, 1)
                    nc.vector.tensor_tensor(Q_sp[:, :, 1, :], work_ps[0][:, B * P:2 * B * P].rearrange("p (b d) -> p b d", b=B),
                                            f32(Q_sp[:, :, 0, :]), ALU.subtract).then_inc(Q_lo_ready, 1)
                if n == PREP + ST_BIAS:
                    dve.wait_ge(prep_mm, ST_BIAS + 1)
                    dve.wait_ge(l3_in[0], 16 * 7)
                    nc.vector.tensor_tensor(cb_row[:, :, :], work_ps[1][:, 0:B * P].rearrange("p (b d) -> p b d", b=B),
                                            row_bias[:, 0:1, 0, :].to_broadcast([P, B, P]), ALU.add).then_inc(cb_row_ready, 1)
                if n == PREP + ST_DNT:
                    dve.wait_ge(downT_hi_ready, 1)
                    for b in range(B):
                        nc.vector.tensor_tensor(downT_sp[:, b, :, 1, :],
                                                work_ps[0][:, b * HC * P:(b + 1) * HC * P].rearrange("p (c d) -> p c d", c=HC),
                                                f32(downT_sp[:, b, :, 0, :]), ALU.subtract).then_inc(downT_lo_ready, 1)
                for b in range(B):
                    if n == PREP + ST_R0 + b:
                        dve.wait_ge(R_hi_ready, b + 1)
                        nc.vector.tensor_tensor(R_lo[:, b, :], work_ps[1 - b][:, :], f32(R_hi[:, b, :]),
                                                ALU.subtract).then_inc(R_lo_ready, 1)

            def hid_high(n):
                dve.wait_ge(hid_ready, n + 1)
                if n >= RING:
                    dve.wait_ge(down_done, n - RING + 1)
                nc.vector.tensor_copy(hid_hi[:, n % RING, :], hid[:, n % RING, :]).then_inc(hid_hi_ready, 1)

            def hid_low(n):
                dve.wait_ge(hid_hi_ready, n + 1)
                if n >= RING:
                    dve.wait_ge(down_done, n - RING + 1)
                nc.vector.tensor_tensor(hid_lo[:, n % RING, :], hid[:, n % RING, :], f32(hid_hi[:, n % RING, :]),
                                        ALU.subtract).then_inc(hid_lo_ready, 1)

            def split_x1(u):
                dve.wait_ge(x1_hi_ready, u + 1)
                nc.vector.tensor_tensor(x1_lo[:, u, :], acc_ps[u][:, :], f32(x1_hi[:, u, :]),
                                        ALU.subtract).then_inc(x1_lo_ready, 1)

            def tail_hid(u, c):
                dve.wait_ge(gate3_ready, HC * u + c + 1)
                dve.wait_ge(silu_ready, HC * u + c + 1)
                if u:
                    dve.wait_ge(hid3_lo_ready, c + 1)
                nc.vector.scalar_tensor_tensor(hid3[:, c, :], tail_banks(u, c)[1][:, :],
                                               ug_bias[:, u, HC + c:HC + c + 1], silu[:, c, :],
                                               ALU.add, ALU.mult).then_inc(hid3_ready, 1)

            def tail_hid_hi(u, c):
                dve.wait_ge(hid3_ready, HC * u + c + 1)
                nc.vector.tensor_copy(hid3_hi[:, u, c, :], hid3[:, c, :]).then_inc(hid3_hi_ready, 1)

            def tail_hid_lo(u, c):
                dve.wait_ge(hid3_hi_ready, HC * u + c + 1)
                if (u, c) == (1, 1):
                    dve.wait_ge(hid3_lo_ready, HC + 1)
                nc.vector.tensor_tensor(hid3_lo[:, u, c, :], hid3[:, c, :], f32(hid3_hi[:, u, c, :]),
                                        ALU.subtract).then_inc(hid3_lo_ready, 1)

            def tail_low_order(k):
                dve.wait_ge(out_ready, k + 1)
                if k == 0:
                    dve.wait_ge(out_bias_ready, B)
                u = k // PAIR
                nc.vector.tensor_tensor(corr[:, k, :, :], out_bank(u, k % PAIR)[:, :, 1, :],
                                        out_bias[:, u, :].unsqueeze(1).to_broadcast([P, PAIR, D]),
                                        ALU.add).then_inc(corr_ready, 1)

            def tail_result(k):
                dve.wait_ge(corr_ready, k + 1)
                u, cols = k // PAIR, slice(k % PAIR * PAIR * D, (k % PAIR + 1) * PAIR * D)
                nc.vector.tensor_tensor(result[:, u, cols].rearrange("p (j d) -> p j d", d=D),
                                        out_bank(u, k % PAIR)[:, :, 0, :], corr[:, k, :, :],
                                        ALU.add).then_inc(result_ready, 1)

            def hidden(n):
                s, b, c = step_parts(n)
                dve.wait_ge(gelu_ready, n + 1)
                dve.wait_ge(up_ready, n + 1)
                if s == 0:
                    op = nc.vector.tensor_tensor(hid[:, n % RING, :], up_ps[n % 2][:, :], gelu[:, n % 2, :], ALU.mult)
                else:
                    k = (s - 1) % TOP
                    if n == B * C:
                        dve.wait_ge(route_step, B + ROUTE_STEPS)
                    op = nc.vector.scalar_tensor_tensor(hid[:, n % RING, :], up_ps[n % 2][:, :], w_route[:, b, k:k + 1],
                                                        gelu[:, n % 2, :], ALU.mult, ALU.mult)
                op.then_inc(hid_ready, 1)

            for n in range(STEPS - 1):
                hidden(n)
                if n == 0:
                    split_shared(DOWN, 0, I)
                    split_x(1)
                if n in DVE_HI:
                    hid_high(n)
                prepare(n)
                if n < PREP + ST_Q:
                    leave_work_banks(n)
                if n == STEPS - 2:
                    hidden(STEPS - 1)
                hid_low(n)
                if n >= PREP + ST_Q:
                    leave_work_banks(n)
                if n == X1_STEP:
                    split_x1(0)
            hid_high(STEPS - 1)
            hid_low(STEPS - 1)
            tail_hid(0, 0)
            tail_hid_hi(0, 0)
            tail_hid_lo(0, 0)
            split_x1(1)
            tail_hid(0, 1)
            tail_hid_lo(0, 1)
            tail_hid(1, 0)
            tail_hid_hi(1, 0)
            tail_hid(1, 1)
            tail_low_order(0)
            tail_low_order(1)
            tail_hid_lo(1, 1)
            tail_result(0)
            tail_result(1)
            tail_low_order(2)
            tail_low_order(3)
            tail_result(2)
            tail_result(3)

        @block.tensor
        def _(pe):
            def product(dst, w_pair, v_pair, start, stop):
                nc.tensor.matmul(dst, w_pair[0], v_pair[0], start=start, stop=False)
                nc.tensor.matmul(dst, w_pair[1], v_pair[0], start=False, stop=False)
                return nc.tensor.matmul(dst, w_pair[0], v_pair[1], start=False, stop=stop)

            def turn_x(b):
                pe.wait_ge(x_in[b], 16)
                for j in range(J):
                    last = nc.tensor.transpose(work_ps[b][:, j * P:(j + 1) * P], x_tok[:, b, j * P:(j + 1) * P], ident[:, :])
                last.then_inc(xT_ready, 1)

            def residual(b):
                pe.wait_ge(xT_hi_ready, b + 1)
                nc.tensor.matmul(acc_ps[b][:, :], ident_r[:, :], xT_hi[:, b, :], start=True, stop=False)
                pe.wait_ge(xT_lo_ready, b + 1)
                nc.tensor.matmul(acc_ps[b][:, :], ident_r[:, :], xT_lo[:, b, :], start=False, stop=False)

            def hidden(n):
                s, b, c = step_parts(n)
                xT = (xT_hi[:, b, :], xT_lo[:, b, :])
                cols = slice(c * P, (c + 1) * P)
                for m, banks, read, done in ((GATE, gate_ps, gelu_ready, gate_ready), (UP, up_ps, hid_ready, up_ready)):
                    dst, w = banks[n % 2][:, :], (w_hi[:, s, m, cols], w_lo[:, s, m, cols])
                    parts = 1 if s or c == 0 else 2
                    if n >= 2:
                        pe.wait_ge(read, n - 1)
                    if c < 2:
                        pe.wait_ge(w_hi_ready[s][m], parts if m == GATE else 1)
                    nc.tensor.matmul(dst, w[0], xT[0], start=True, stop=False)
                    if c < 2:
                        pe.wait_ge(w_lo_ready[s][m], parts)
                    nc.tensor.matmul(dst, w[1], xT[0], start=False, stop=False)
                    if c == 0 and s == 0:
                        pe.wait_ge(xT_lo_ready, b + 1)
                    nc.tensor.matmul(dst, w[0], xT[1], start=False, stop=True).then_inc(done, 1)

            def down(n):
                s, b, c = step_parts(n)
                cols = slice(c * P, (c + 1) * P)
                if c == 0:
                    pe.wait_ge(w_hi_ready[s][DOWN], 1)
                    pe.wait_ge(w_lo_ready[s][DOWN], 1)
                closes = n + 1 in (FIRST_STEPS, STEPS)
                w_h, w_l = w_hi[:, s, DOWN, cols], w_lo[:, s, DOWN, cols]
                pe.wait_ge(hid_hi_ready, n + 1)
                nc.tensor.matmul(acc_ps[b][:, :], w_h, hid_hi[:, n % RING, :], start=False, stop=False)
                nc.tensor.matmul(acc_ps[b][:, :], w_l, hid_hi[:, n % RING, :], start=False, stop=False)
                pe.wait_ge(hid_lo_ready, n + 1)
                nc.tensor.matmul(acc_ps[b][:, :], w_h, hid_lo[:, n % RING, :], start=False,
                                 stop=closes).then_inc(down_done, 1)

            def prepare(n):
                if n == PREP + ST_BS:
                    pe.wait_ge(l1_in, 16 * 4)
                    pe.wait_ge(xT_lo_ready, B)
                    pe.wait_ge(bs_mix_ready, B)
                    for b in range(B):
                        last = nc.tensor.transpose(work_ps[0][:, b * P:(b + 1) * P],
                                                   bs_mix[:, b, :, :].rearrange("o e r -> o (e r)"), ident[:, :])
                    last.then_inc(prep_mm, 1)
                if n == PREP + ST_A:
                    pe.wait_ge(bsT_ready, 1)
                    for b in range(B):
                        nc.tensor.matmul(work_ps[1][:, b * P:(b + 1) * P], bsT[:, b, :], as_sb[:, :], start=True, stop=True)
                    pe.wait_ge(masked_ready, 1)
                    for b in range(B):
                        last = nc.tensor.transpose(work_ps[0][:, (B + b) * P:(B + b + 1) * P], mix_masked[:, b, :], ident[:, :])
                    last.then_inc(prep_mm, 1)
                if n == PREP + ST_Q:
                    pe.wait_ge(A2_ready, 1)
                    pe.wait_ge(A1T_ready, 1)
                    for b in range(B):
                        nc.tensor.matmul(work_ps[0][:, b * P:(b + 1) * P], A2[:, b, :], A1T[:, b, :], start=True, stop=True)
                    for b in range(B):
                        last = nc.tensor.matmul(work_ps[0][:, (B + b) * P:(B + b + 1) * P], A1T[:, b, :], A2[:, b, :],
                                                start=True, stop=True)
                    last.then_inc(prep_mm, 1)
                if n == PREP + ST_BIAS:
                    pe.wait_ge(b1_wide_ready, 1)
                    nc.tensor.matmul(work_ps[1][:, 0:B * P], b1_wide[:, :], A2[:, :, :].rearrange("p b d -> p (b d)"),
                                     start=True, stop=True).then_inc(prep_mm, 1)
                if n in (PREP + ST_UGT0, PREP + ST_UGT1):
                    b = n - PREP - ST_UGT0
                    pe.wait_ge(l3_in[b], 16 * 7)
                    if b == 0:
                        pe.wait_ge(QT_ready, 1)
                        pe.wait_ge(Q_lo_ready, 1)
                    else:
                        pe.wait_ge(cb_row_ready, 1)
                    for k in range(2 * HC):
                        last = nc.tensor.transpose(work_ps[b][:, k * P:(k + 1) * P], upgate_raw[:, b, k, :], ident[:, :])
                    last.then_inc(prep_mm, 1)
                if n == PREP + ST_DNT:
                    pe.wait_ge(upgateT_ready, 1)
                    for b in range(B):
                        for c in range(HC):
                            k = b * HC + c
                            last = nc.tensor.transpose(work_ps[0][:, k * P:(k + 1) * P], down_raw[:, b, :, c], ident[:, :])
                    last.then_inc(prep_mm, 1)
                if n in (PREP + ST_R0, PREP + ST_R1):
                    b = n - PREP - ST_R0
                    pe.wait_ge(upgateT_ready, B)
                    if b == 1:
                        pe.wait_ge(downT_lo_ready, B)
                    nc.tensor.matmul(work_ps[1 - b][:, :], QT[:, b, :], upgateT[:, b, :], start=True,
                                     stop=True).then_inc(prep_mm, 1)

            def tail_up_gate(u, c):
                up, gate = tail_banks(u, c)
                x1 = (x1_hi[:, u, :], x1_lo[:, u, :])
                if c == 0:
                    pe.wait_ge(x1_hi_ready, u + 1)
                    pe.wait_ge(x1_lo_ready, u + 1)
                if (u, c) == (0, 0):
                    pe.wait_ge(R_lo_ready, B)
                if (u, c) == (0, 1):
                    pe.wait_ge(gelu_ready, STEPS - 1)
                    pe.wait_ge(hid_ready, STEPS - 1)
                if (u, c) == (1, 0):
                    pe.wait_ge(gelu_ready, STEPS)
                if (u, c) == (1, 1):
                    pe.wait_ge(hid3_ready, 1)
                for dst, k, done in ((up, c, up3_ready), (gate, HC + c, gate3_ready)):
                    cols = slice(k * P, (k + 1) * P)
                    product(dst[:, :], (R_hi[:, u, cols], R_lo[:, u, cols]), x1, True, True).then_inc(done, 1)

            def out_tiles(u, v_hi, v_lo, w_sp, start, stop, ready=None):
                for j in range(J):
                    k, first, last = j // PAIR, j % PAIR == 0, j % PAIR == PAIR - 1
                    tile, cols = out_bank(u, k)[:, j % PAIR, :, :], slice(j * P, (j + 1) * P)
                    nc.tensor.matmul(tile, v_hi[:, cols], w_sp, start=start and first, stop=False)
                    mm = nc.tensor.matmul(tile[:, 1, :], v_lo[:, cols], w_sp[:, 0, :], start=False, stop=stop and last)
                    if ready and last:
                        mm.then_inc(ready, 1)

            def tail_residual(u):
                if u == 0:
                    pe.wait_ge(Q_lo_ready, 1)
                    pe.wait_ge(x1_lo_ready, 1)
                    pe.wait_ge(hid_ready, STEPS)
                else:
                    pe.wait_ge(hid3_ready, 2)
                out_tiles(u, x1_hi[:, u, :], x1_lo[:, u, :], Q_sp[:, u, :, :], True, False)

            def tail_down(u, c):
                pe.wait_ge(hid3_hi_ready, HC * u + c + 1)
                pe.wait_ge(hid3_lo_ready, HC * u + c + 1)
                if (u, c) == (0, 0):
                    pe.wait_ge(downT_lo_ready, B)
                end = c == HC - 1
                out_tiles(u, hid3_hi[:, u, c, :], hid3_lo[:, u, c, :], downT_sp[:, u, c, :, :], False, end,
                          out_ready if end else None)

            def warm_up(count):
                for _ in range(count):
                    nc.tensor.matmul(gate_ps[1][:, 0:P], ident[:, :], ident[:, :], start=True, stop=True)

            pe.wait_ge(ident_ready, 1)
            warm_up(WARM_BEFORE_X)
            turn_x(0)
            warm_up(WARM_AFTER_X)
            pe.wait_ge(ident_ready, 2)
            pe.wait_ge(xT_hi_ready, 1)
            for n in range(STEPS):
                hidden(n)
                if n == 0:
                    turn_x(1)
                    residual(0)
                if n == 1:
                    residual(1)
                if n >= LAG:
                    down(n - LAG)
                prepare(n)
            tail_up_gate(0, 0)
            tail_residual(0)
            down(STEPS - 2)
            down(STEPS - 1)
            tail_up_gate(0, 1)
            tail_down(0, 0)
            tail_up_gate(1, 0)
            tail_up_gate(1, 1)
            tail_down(0, 1)
            tail_residual(1)
            tail_down(1, 0)
            tail_down(1, 1)


_INS = ['x', 'cond_8', 'L0_cond_skill_gate', 'L0_cond_skill_up', 'L0_cond_skill_down', 'L0_cond_shared_gate',
        'L0_cond_shared_up', 'L0_cond_shared_down', 'L1_cond_W_base', 'L1_cond_b_base', 'L1_cond_As', 'L1_cond_Bs',
        'L2_cond_weight', 'L2_cond_mask', 'L2_cond_bias', 'L3_cond_W_up', 'L3_cond_b_up', 'L3_cond_W_gate',
        'L3_cond_b_gate', 'L3_cond_W_down', 'L3_cond_b_down']


def kernel(**inputs):
    import numpy as _np
    import concourse.bacc as _bacc
    from concourse import mybir as _mybir
    from concourse.bass_utils import run_bass_kernel_spmd as _run

    nc = _bacc.Bacc("TRN2", target_bir_lowering=False, num_devices=1)
    arrays, args = {}, []
    for name in _INS:
        a = _np.ascontiguousarray(inputs[name])
        arrays[f"in_{name}_dram"] = a
        args.append(nc.dram_tensor(f"in_{name}_dram", a.shape, _mybir.dt.from_np(a.dtype), kind="ExternalInput").ap())
    out = nc.dram_tensor("out_0_dram", inputs["x"].shape, _mybir.dt.from_np(_np.dtype("float32")), kind="ExternalOutput").ap()
    build(nc, *args, out)
    r = _run(nc, [arrays], core_ids=[0])
    return r.results[0]["out_0_dram"]
```

```python
import concourse.bass as bass
from concourse import mybir
from contextlib import ExitStack


def build(nc, x, cond, sk_gate, sk_up, sk_down, sh_gate, sh_up, sh_down, W_base, b_base, As, Bs,
          weight, mask, bias, W_up, b_up, W_gate, b_gate, W_down, b_down, out):
    F32, F32R, U32 = mybir.dt.float32, mybir.dt.float32r, mybir.dt.uint32
    ALU, ACT, AX = mybir.AluOpType, mybir.ActivationFunctionType, mybir.AxisListType

    B, S, D = x.shape
    E, _, I = sk_gate.shape
    R = As.shape[1]
    H = W_up.shape[1]
    P = 128
    J = S // P
    C = I // P
    HC = H // P
    TOP = 2
    LORA_SCALE = 32.0 / R
    ROUTE_SCALE = 1.0 / 12
    assert D == P and E * R == P and E == 8

    BLOCKS = [(0, 0), (0, 1)] + [(1 + TOP * b + k, b) for b in range(B) for k in range(TOP)]
    SETS = 1 + TOP * B
    STEPS = len(BLOCKS) * C
    FIRST_STEPS = (B + TOP) * C
    LAG = 2
    GATE, UP, DOWN = range(3)
    RING = 3

    WARM_BEFORE_X, WARM_AFTER_X = 4, 2
    ROUTE_STEPS = 5
    FOLDS = [P >> k for k in range(1, P.bit_length())]
    EXPERT = 2
    MIX = 3
    PREP = MIX + E + 1
    PAIR = 2
    OUT_PARTS = B * J // PAIR
    X1_STEP = PREP + 10
    assert X1_STEP >= FIRST_STEPS - 1 + LAG

    ctx = ExitStack()
    with ctx:
        def sb(name, shape, dt=F32):
            return ctx.enter_context(nc.sbuf_tensor(name, shape, dt))

        def ps(name):
            return ctx.enter_context(nc.psum_tensor(name, [P, 512], F32))

        def sem(name):
            return ctx.enter_context(nc.semaphore(name))

        ident = sb("ident", [P, P])
        cond_all = sb("cond_all", [P, B, E])
        top_val = sb("top_val", [P, B, 8])
        top_idx = sb("top_idx", [P, B, 8], U32)
        neg_max = sb("neg_max", [P, B])
        top_exp = sb("top_exp", [P, B, TOP])
        exp_sum = sb("exp_sum", [P, B, 1])
        exp_inv = sb("exp_inv", [P, B, 1])
        w_norm = sb("w_norm", [P, B, TOP])
        w_stop = sb("w_stop", [P, B, TOP])
        w_route = sb("w_route", [P, B, TOP])
        x_tok = sb("x_tok", [P, B, S])
        xT_hi = sb("xT_hi", [P, B, S], F32R)
        xT_lo = sb("xT_lo", [P, B, S], F32R)
        w_raw = sb("w_raw", [P, SETS, 3, I])
        w_hi = sb("w_hi", [P, SETS, 3, I], F32R)
        w_lo = sb("w_lo", [P, SETS, 3, I], F32R)
        gelu = sb("gelu", [P, 2, S])
        hid = sb("hid", [P, RING, S])
        hid_hi = sb("hid_hi", [P, RING, S], F32R)
        hid_lo = sb("hid_lo", [P, RING, S], F32R)
        base_sb = sb("base_sb", [P, P])
        b1_col = sb("b1_col", [P, 1])
        b1_wide = sb("b1_wide", [P, P])
        as_sb = sb("as_sb", [P, P])
        bs_sb = sb("bs_sb", [P, E, R])
        bs_mix = sb("bs_mix", [P, B, E, R])
        bsT = sb("bsT", [P, B, P])
        mix_w = sb("mix_w", [P, E, P])
        mask_sb = sb("mask_sb", [P, P])
        mix_acc = sb("mix_acc", [P, B, P])
        A1T = sb("A1T", [P, B, P])
        A2 = sb("A2", [P, B, P])
        QT_hi = sb("QT_hi", [P, B, P], F32R)
        QT_lo = sb("QT_lo", [P, B, P], F32R)
        Q_sp = sb("Q_sp", [P, B, 2, P], F32R)
        cb_row = sb("cb_row", [P, B, P])
        upgate_raw = sb("upgate_raw", [P, B, 2 * HC, P])
        down_raw = sb("down_raw", [P, B, P, HC])
        bug_col = sb("bug_col", [P, B, 2, HC])
        row_bias = sb("row_bias", [P, B, 2, P])
        bias_prod = sb("bias_prod", [P, B, 2 * HC, P])
        out_bias = sb("out_bias", [P, B, P])
        upgateT_hi = sb("upgateT_hi", [P, B, 2 * HC * P], F32R)
        upgateT_lo = sb("upgateT_lo", [P, B, 2 * HC * P], F32R)
        downT_sp = sb("downT_sp", [P, B, HC, 2, P], F32R)
        R_hi = sb("R_hi", [P, B, 2 * HC * P], F32R)
        R_lo = sb("R_lo", [P, B, 2 * HC * P], F32R)
        ug_bias = sb("ug_bias", [P, B, 2 * HC])
        x1_hi = sb("x1_hi", [P, B, S], F32R)
        x1_lo = sb("x1_lo", [P, B, S], F32R)
        silu = sb("silu", [P, HC, S])
        hid3 = sb("hid3", [P, HC, S])
        hid3_hi = sb("hid3_hi", [P, B, HC, S], F32R)
        hid3_lo = sb("hid3_lo", [P, B, HC, S], F32R)
        result = gelu
        zeros = sb("zeros", [P, P], F32R)
        table_scratch = sb("table_scratch", [P, 4])

        gate_ps = [ps("gate_ps0"), ps("gate_ps1")]
        up_ps = [ps("up_ps0"), ps("up_ps1")]
        acc_ps = [ps("acc_ps0"), ps("acc_ps1")]
        work_ps = [ps("work_ps0"), ps("work_ps1")]

        cond_in = sem("cond_in")
        x_in = [(sem("x_in0_first"), sem("x_in0_second")), (sem("x_in1"),)]
        w_in = [[sem(f"w_in{s}_{m}") for m in range(3)] for s in range(SETS)]
        l1_in, l2_in = sem("l1_in"), sem("l2_in")
        l3_in = [sem(f"l3_in{b}") for b in range(B)]
        stored = [sem(f"stored{k}") for k in range(OUT_PARTS)]
        ident_set, ident_ready = sem("ident_set"), sem("ident_ready")
        bs_mix_ready = sem("bs_mix_ready")
        base_ready, b1_wide_ready = sem("base_ready"), sem("b1_wide_ready")
        top_found, neg_max_ready, top_exp_ready = sem("top_found"), sem("neg_max_ready"), sem("top_exp_ready")
        route_step = sem("route_step")
        zeros_ready = sem("zeros_ready")
        scratch_ready, tables_loaded = sem("scratch_ready"), sem("tables_loaded")
        xT_ready, xT_hi_ready, xT_lo_ready = sem("xT_ready"), sem("xT_hi_ready"), sem("xT_lo_ready")
        w_hi_ready = [[sem(f"w_hi_ready{s}_{m}") for m in range(3)] for s in range(SETS)]
        w_lo_ready = [[sem(f"w_lo_ready{s}_{m}") for m in range(3)] for s in range(SETS)]
        gate_ready, up_ready, down_done = sem("gate_ready"), sem("up_ready"), sem("down_done")
        gelu_ready, hid_ready = sem("gelu_ready"), sem("hid_ready")
        hid_hi_ready, hid_lo_ready = sem("hid_hi_ready"), sem("hid_lo_ready")
        mix_step, masked_ready = sem("mix_step"), sem("masked_ready")
        prep_mm = sem("prep_mm")
        bsT_ready, A2_ready, A1T_ready = sem("bsT_ready"), sem("A2_ready"), sem("A1T_ready")
        QT_hi_ready, QT_lo_ready = sem("QT_hi_ready"), sem("QT_lo_ready")
        Q_hi_ready, Q_lo_ready = sem("Q_hi_ready"), sem("Q_lo_ready")
        cb_row_ready, out_bias_ready = sem("cb_row_ready"), sem("out_bias_ready")
        bias_fold = [sem(f"bias_fold{b}") for b in range(B)]
        upgateT_hi_ready, upgateT_lo_ready = sem("upgateT_hi_ready"), sem("upgateT_lo_ready")
        downT_hi_ready, downT_lo_ready = sem("downT_hi_ready"), sem("downT_lo_ready")
        R_hi_ready, R_lo_ready = sem("R_hi_ready"), sem("R_lo_ready")
        ug_bias_ready = sem("ug_bias_ready")
        x1_hi_ready, x1_lo_ready = sem("x1_hi_ready"), sem("x1_lo_ready")
        up3_ready, gate3_ready = sem("up3_ready"), sem("gate3_ready")
        silu_ready, hid3_ready = sem("silu_ready"), sem("hid3_ready")
        hid3_hi_ready, hid3_lo_ready = sem("hid3_hi_ready"), sem("hid3_lo_ready")
        out_ready, corr_ready, result_ready = sem("out_ready"), sem("corr_ready"), sem("result_ready")

        (ST_BS, ST_A, ST_Q, ST_BIAS, ST_UGT0, ST_UGT1, ST_DNT, ST_R0, ST_R1) = range(9)

        def f32(ap):
            return ap.bitcast(F32)

        def corr(k):
            return mix_w[:, k * PAIR:(k + 1) * PAIR, :]

        def step_parts(n):
            s, b = BLOCKS[n // C]
            return s, b, n % C

        def tail_banks(u, c):
            return {(0, 0): work_ps, (0, 1): (up_ps[0], gate_ps[0]),
                    (1, 0): (acc_ps[1], gate_ps[1]), (1, 1): work_ps}[u, c]

        def out_bank(u, k):
            return ((acc_ps[0], up_ps[1]), (up_ps[0], gate_ps[0]))[u][k][:, :].rearrange("p (j m d) -> p j m d", j=PAIR, m=2)

        block = ctx.enter_context(nc.Block())

        @block.sync
        def _(sp):
            def load_x(b, lo, hi):
                sp.dma_start(x_tok[:, b, lo * P:hi * P],
                             x[b, :, :].rearrange("(p j) d -> p (j d)", j=J)[:, lo * D:hi * D]).then_inc(x_in[b][lo * 2 // J], 16)

            load_x(0, 0, J // 2)
            load_x(0, J // 2, J)
            sp.dma_start(cond_all[:, :, :], cond.rearrange("b e -> (b e)").partition_broadcast(P)).then_inc(cond_in, 16)
            sp.dma_start(w_raw[:, 0, GATE, :], sh_gate).then_inc(w_in[0][GATE], 16)
            sp.dma_start(w_raw[:, 0, UP, :], sh_up).then_inc(w_in[0][UP], 16)
            load_x(1, 0, J)
            sp.dma_start(w_raw[:, 0, DOWN, :].rearrange("p (c h) -> p c h", c=C),
                         sh_down.rearrange("(c p) h -> p c h", p=P)).then_inc(w_in[0][DOWN], 16)

            def load_expert(s, e):
                one = bass.ds(e, 1)
                for m, w in ((GATE, sk_gate), (UP, sk_up)):
                    sp.dma_start(w_raw[:, s, m, :], w[one, :, :].rearrange("e h i -> h (e i)")).then_inc(w_in[s][m], 16)
                sp.dma_start(w_raw[:, s, DOWN, :].rearrange("p (c h) -> p c h", c=C),
                             sk_down[one, :, :].rearrange("e (c p) h -> p (e c) h", p=P)).then_inc(w_in[s][DOWN], 16)

            def load_l3(b, e):
                one = bass.ds(e, 1)
                for m, w in ((0, W_up), (1, W_gate)):
                    sp.dma_start(upgate_raw[:, b, m * HC:(m + 1) * HC, :],
                                 w[one, :, :].rearrange("e (p c) d -> p (e c) d", c=HC)).then_inc(l3_in[b], 16)
                sp.dma_start(down_raw[:, b, :, :],
                             W_down[one, :, :].rearrange("e d (p c) -> d (e p) c", c=HC)).then_inc(l3_in[b], 16)
                for m, v in ((0, b_up), (1, b_gate)):
                    sp.dma_start(bug_col[:, b, m, :],
                                 v[one, :].rearrange("e (p c) -> p (e c)", c=HC)).then_inc(l3_in[b], 16)
                sp.dma_start(row_bias[:, b, 1, :],
                             b_down[one, :].rearrange("e d -> (e d)").partition_broadcast(P)).then_inc(l3_in[b], 16)

            sp.wait_ge(top_found, B)
            first = [sp.value_load(top_idx[0:1, b, 0:1], min_val=0, max_val=E - 1) for b in range(B)]
            second = [sp.value_load(top_idx[0:1, b, 1:2], min_val=0, max_val=E - 1) for b in range(B)]
            load_expert(1, first[0])
            with nc.allow_non_contiguous_dma(reason="128 single values"):
                sp.dma_start(b1_col[:, :], b_base.rearrange("(o a) -> o a", a=1)).then_inc(l1_in, 16)
            sp.dma_start(as_sb[:, :], As.rearrange("e r c -> (e r) c")).then_inc(l1_in, 16)
            sp.dma_start(bs_sb[:, :, :], Bs.rearrange("e o r -> o e r")).then_inc(l1_in, 16)
            sp.dma_start(base_sb[:, :], W_base).then_inc(l1_in, 16)
            sp.dma_start(mix_w[:, :, :], weight.rearrange("g o t -> o g t")).then_inc(l2_in, 16)
            sp.dma_start(mask_sb[:, :], mask).then_inc(l2_in, 16)
            load_expert(2, second[0])
            for b in range(B):
                sp.dma_start(row_bias[:, b, 0, :], bias.partition_broadcast(P)).then_inc(l3_in[b], 16)
                load_l3(b, first[b])
            load_expert(3, first[1])
            load_expert(4, second[1])
            for k in range(OUT_PARTS):
                u, lo = k // PAIR, k % PAIR * PAIR * D
                sp.wait_ge(result_ready, k + 1)
                sp.dma_start(out[u, :, :].rearrange("(p j) d -> p (j d)", j=J)[:, lo:lo + PAIR * D],
                             result[:, u, lo:lo + PAIR * D]).then_inc(stored[k], 16)
            for k in range(OUT_PARTS):
                sp.wait_ge(stored[k], 16)

        @block.gpsimd
        def _(pool):
            nc.gpsimd.memset(ident[:, :], 0.0).then_inc(ident_set, 1)
            pool.wait_ge(ident_set, 1)
            nc.gpsimd.affine_select(out=ident[:, :], in_=ident[:, :], compare_op=ALU.not_equal, fill=1.0, base=0,
                                    pattern=[[-1, P]], channel_multiplier=1).then_inc(ident_ready, 1)

            def split_weight(s, m):
                pool.wait_ge(w_hi_ready[s][m], 1)
                nc.gpsimd.tensor_tensor(w_lo[:, s, m, :], w_raw[:, s, m, :], f32(w_hi[:, s, m, :]),
                                        ALU.subtract).then_inc(w_lo_ready[s][m], 1)

            split_weight(0, DOWN)
            for m in range(3):
                split_weight(1, m)
            pool.wait_ge(l1_in, 16 * 4)
            pool.wait_ge(cond_in, 16)
            for b in range(B):
                nc.gpsimd.tensor_tensor(bs_mix[:, b, :, :], bs_sb[:, :, :],
                                        cond_all[:, b, :].unsqueeze(2).to_broadcast([P, E, R]),
                                        ALU.mult).then_inc(bs_mix_ready, 1)
            nc.gpsimd.tensor_tensor(base_sb[:, :], base_sb[:, :], ident[:, :], ALU.add).then_inc(base_ready, 1)
            nc.gpsimd.tensor_copy(b1_wide[:, :], b1_col[:, 0:1].to_broadcast([P, P])).then_inc(b1_wide_ready, 1)
            for m in range(3):
                split_weight(2, m)
            for s in range(3, SETS):
                for m in range(3):
                    split_weight(s, m)
            pool.wait_ge(cb_row_ready, 1)
            for b in range(B):
                pool.wait_ge(l3_in[b], 16 * 7)
                nc.gpsimd.tensor_tensor(bias_prod[:, b, :, :], upgate_raw[:, b, :, :],
                                        cb_row[:, b, :].unsqueeze(1).to_broadcast([P, 2 * HC, P]),
                                        ALU.mult).then_inc(bias_fold[b], 1)
                nc.gpsimd.tensor_tensor(out_bias[:, b, :], cb_row[:, b, :], row_bias[:, b, 1, :],
                                        ALU.add).then_inc(out_bias_ready, 1)
            for fold, half in enumerate(FOLDS):
                for b in range(B):
                    pool.wait_ge(bias_fold[b], fold + 1)
                    nc.gpsimd.tensor_tensor(bias_prod[:, b, :, 0:half], bias_prod[:, b, :, 0:half],
                                            bias_prod[:, b, :, half:2 * half], ALU.add).then_inc(bias_fold[b], 1)
            for b in range(B):
                pool.wait_ge(bias_fold[b], len(FOLDS) + 1)
                nc.gpsimd.tensor_tensor(ug_bias[:, b, :], bias_prod[:, b, :, 0], bug_col[:, b, :, :].rearrange("p m c -> p (m c)"),
                                        ALU.add).then_inc(ug_bias_ready, 1)
            pool.wait_ge(hid3_hi_ready, HC + 1)
            nc.gpsimd.tensor_tensor(hid3_lo[:, 1, 0, :], hid3[:, 0, :], f32(hid3_hi[:, 1, 0, :]),
                                    ALU.subtract).then_inc(hid3_lo_ready, 1)

        @block.scalar
        def _(act):
            def route_exp():
                act.wait_ge(neg_max_ready, 1)
                for b in range(B):
                    nc.scalar.activation(top_exp[:, b, :], top_val[:, b, 0:TOP], ACT.Exp,
                                         bias=neg_max[:, b:b + 1]).then_inc(top_exp_ready, 1)

            def split_x(b):
                act.wait_ge(xT_ready, b + 1)
                nc.scalar.activation(xT_hi[:, b, :], acc_ps[b][:, :], ACT.Copy).then_inc(xT_hi_ready, 1)

            def split_weight(s, m):
                act.wait_ge(w_in[s][m], 16)
                nc.scalar.activation(w_hi[:, s, m, :], w_raw[:, s, m, :], ACT.Copy).then_inc(w_hi_ready[s][m], 1)

            act.wait_ge(scratch_ready, 1)
            nc.scalar.activation(table_scratch[:, 1:2], table_scratch[:, 0:1], ACT.Exp).then_inc(tables_loaded, 1)
            split_x(0)
            route_exp()
            nc.scalar.activation(table_scratch[:, 2:3], table_scratch[:, 0:1], ACT.Gelu_apprx_tanh).then_inc(tables_loaded, 1)
            act.wait_ge(w_hi_ready[0][UP], 1)
            nc.scalar.activation(w_hi[:, 0, UP, P:I], w_raw[:, 0, UP, P:I], ACT.Copy).then_inc(w_hi_ready[0][UP], 1)

            def prepare(n):
                if n == PREP + ST_BS:
                    act.wait_ge(prep_mm, ST_BS + 1)
                    nc.scalar.activation(bsT[:, :, :], work_ps[0][:, 0:B * P], ACT.Copy, scale=LORA_SCALE).then_inc(bsT_ready, 1)
                k = n - EXPERT
                if 0 <= k < 3 * (SETS - 1):
                    split_weight(1 + k // 3, k % 3)

            def leave_work_banks(n):
                if n == PREP + ST_Q:
                    act.wait_ge(prep_mm, ST_Q + 1)
                    nc.scalar.activation(QT_hi[:, :, :], work_ps[0][:, 0:B * P], ACT.Copy).then_inc(QT_hi_ready, 1)
                    nc.scalar.activation(Q_sp[:, :, 0, :], work_ps[0][:, B * P:2 * B * P].rearrange("p (b d) -> p b d", b=B),
                                         ACT.Copy).then_inc(Q_hi_ready, 1)
                for b in range(B):
                    if n == PREP + ST_UGT0 + b:
                        act.wait_ge(prep_mm, ST_UGT0 + b + 1)
                        nc.scalar.activation(upgateT_hi[:, b, :], work_ps[b][:, :], ACT.Copy).then_inc(upgateT_hi_ready, 1)
                if n == PREP + ST_DNT:
                    act.wait_ge(prep_mm, ST_DNT + 1)
                    nc.scalar.activation(downT_sp[:, :, :, 0, :], work_ps[0][:, :].rearrange("p (b c d) -> p b c d", b=B, c=HC),
                                         ACT.Copy).then_inc(downT_hi_ready, 1)
                for b in range(B):
                    if n == PREP + ST_R0 + b:
                        act.wait_ge(prep_mm, ST_R0 + b + 1)
                        nc.scalar.activation(R_hi[:, b, :], work_ps[1 - b][:, :], ACT.Copy).then_inc(R_hi_ready, 1)

            def split_x1(u):
                if u == 0:
                    act.wait_ge(down_done, FIRST_STEPS)
                else:
                    act.wait_ge(down_done, STEPS)
                nc.scalar.activation(x1_hi[:, u, :], acc_ps[u][:, :], ACT.Copy).then_inc(x1_hi_ready, 1)

            def tail_silu(u, c):
                act.wait_ge(up3_ready, HC * u + c + 1)
                if (u, c) == (0, 0):
                    act.wait_ge(ug_bias_ready, B)
                if u:
                    act.wait_ge(hid3_ready, c + 1)
                nc.scalar.activation(silu[:, c, :], tail_banks(u, c)[0][:, :], ACT.Silu,
                                     bias=ug_bias[:, u, c:c + 1]).then_inc(silu_ready, 1)

            def tail_hid_hi(u, c):
                act.wait_ge(hid3_ready, HC * u + c + 1)
                nc.scalar.activation(hid3_hi[:, u, c, :], hid3[:, c, :], ACT.Copy).then_inc(hid3_hi_ready, 1)

            def gelu_gate(n):
                act.wait_ge(gate_ready, n + 1)
                if n >= 2:
                    act.wait_ge(hid_ready, n - 1)
                nc.scalar.activation(gelu[:, n % 2, :], gate_ps[n % 2][:, :], ACT.Gelu_apprx_tanh).then_inc(gelu_ready, 1)

            def hid_high(n):
                act.wait_ge(hid_ready, n + 1)
                if n >= RING:
                    act.wait_ge(down_done, n - RING + 1)
                nc.scalar.activation(hid_hi[:, n % RING, :], hid[:, n % RING, :], ACT.Copy).then_inc(hid_hi_ready, 1)

            for n in range(STEPS):
                gelu_gate(n)
                if n == 0:
                    split_x(1)
                if n:
                    hid_high(n - 1)
                    leave_work_banks(n - 1)
                prepare(n)
                if n == X1_STEP:
                    split_x1(0)
            act.wait_ge(ug_bias_ready, B)
            nc.scalar.activation(table_scratch[:, 3:4], ug_bias[:, 0, 0:1], ACT.Silu).then_inc(tables_loaded, 1)
            tail_silu(0, 0)
            split_x1(1)
            tail_silu(0, 1)
            tail_hid_hi(0, 1)
            tail_silu(1, 0)
            tail_silu(1, 1)
            tail_hid_hi(1, 1)

        @block.vector
        def _(dve):
            nc.vector.memset(zeros[:, :].bitcast(F32), 0.0).then_inc(zeros_ready, 1)
            nc.vector.memset(table_scratch[:, 0:1], 0.0).then_inc(scratch_ready, 1)
            def route_weights(step):
                if step == 0:
                    dve.wait_ge(top_exp_ready, B)
                    op = nc.vector.tensor_tensor(exp_sum[:, :, :], top_exp[:, :, 0:1], top_exp[:, :, 1:2], ALU.add)
                else:
                    dve.wait_ge(route_step, B + step)
                if step == 1:
                    op = nc.vector.reciprocal(exp_inv[:, :, :], exp_sum[:, :, :])
                if step == 2:
                    op = nc.vector.tensor_tensor(w_norm[:, :, :], top_exp[:, :, :], exp_inv[:, :, :].to_broadcast([P, B, TOP]), ALU.mult)
                if step == 3:
                    op = nc.vector.tensor_scalar(w_stop[:, :, :], w_norm[:, :, :], 1.0 - ROUTE_SCALE, None, ALU.mult)
                if step == 4:
                    op = nc.vector.scalar_tensor_tensor(w_route[:, :, :], w_norm[:, :, :], ROUTE_SCALE, w_stop[:, :, :],
                                                        ALU.mult, ALU.add)
                op.then_inc(route_step, 1)

            def split_x(b):
                dve.wait_ge(xT_hi_ready, b + 1)
                nc.vector.tensor_tensor(xT_lo[:, b, :], acc_ps[b][:, :], f32(xT_hi[:, b, :]),
                                        ALU.subtract).then_inc(xT_lo_ready, 1)

            def shared_hi(m, lo, hi):
                dve.wait_ge(w_in[0][m], 16)
                nc.vector.tensor_copy(w_hi[:, 0, m, lo:hi], w_raw[:, 0, m, lo:hi]).then_inc(w_hi_ready[0][m], 1)

            def shared_lo(m, lo, hi):
                dve.wait_ge(w_hi_ready[0][m], 1 if lo == 0 else 2)
                nc.vector.tensor_tensor(w_lo[:, 0, m, lo:hi], w_raw[:, 0, m, lo:hi], f32(w_hi[:, 0, m, lo:hi]),
                                        ALU.subtract).then_inc(w_lo_ready[0][m], 1)

            dve.wait_ge(cond_in, 16)
            for b in range(B):
                nc.vector.max(top_val[:, b, :], cond_all[:, b, :]).then_inc(route_step, 1)
            dve.wait_ge(route_step, B)
            nc.vector.tensor_scalar(neg_max[:, :], top_val[:, :, 0], -1.0, None, ALU.mult).then_inc(neg_max_ready, 1)
            for b in range(B):
                nc.vector.max_index(top_idx[:, b, :], top_val[:, b, :], cond_all[:, b, :]).then_inc(top_found, 1)
            shared_hi(GATE, 0, P)
            shared_lo(GATE, 0, P)
            split_x(0)
            shared_hi(UP, 0, P)
            shared_lo(UP, 0, P)
            shared_hi(GATE, P, I)
            shared_lo(GATE, P, I)
            shared_lo(UP, P, I)
            shared_hi(DOWN, 0, I)

            def mix(g):
                for b in range(B):
                    y = cond_all[:, b, g:g + 1]
                    if g == 0:
                        dve.wait_ge(l2_in, 16 * 2)
                        op = nc.vector.tensor_scalar(mix_acc[:, b, :], mix_w[:, g, :], y, None, ALU.mult)
                    else:
                        dve.wait_ge(mix_step, B * (g - 1) + b + 1)
                        op = nc.vector.scalar_tensor_tensor(mix_acc[:, b, :], mix_w[:, g, :], y, mix_acc[:, b, :],
                                                            ALU.mult, ALU.add)
                    op.then_inc(mix_step, 1)

            def prepare(n):
                if 1 <= n <= ROUTE_STEPS:
                    route_weights(n - 1)
                if MIX <= n < MIX + E:
                    mix(n - MIX)
                if n == MIX + E:
                    dve.wait_ge(mix_step, B * E)
                    nc.vector.tensor_tensor(mix_acc[:, :, :], mix_acc[:, :, :],
                                            mask_sb[:, :].unsqueeze(1).to_broadcast([P, B, P]),
                                            ALU.mult).then_inc(masked_ready, 1)

            def leave_work_banks(n):
                if n == PREP + ST_A:
                    dve.wait_ge(prep_mm, ST_A + 1)
                    nc.vector.tensor_tensor(A2[:, :, :], work_ps[0][:, B * P:2 * B * P].rearrange("p (b o) -> p b o", b=B),
                                            ident[:, :].unsqueeze(1).to_broadcast([P, B, P]),
                                            ALU.add).then_inc(A2_ready, 1)
                    dve.wait_ge(base_ready, 1)
                    nc.vector.tensor_tensor(A1T[:, :, :], work_ps[1][:, 0:B * P].rearrange("p (b c) -> p b c", b=B),
                                            base_sb[:, :].unsqueeze(1).to_broadcast([P, B, P]),
                                            ALU.add).then_inc(A1T_ready, 1)
                if n == PREP + ST_Q:
                    dve.wait_ge(QT_hi_ready, 1)
                    dve.wait_ge(Q_hi_ready, 1)
                    nc.vector.tensor_tensor(QT_lo[:, :, :], work_ps[0][:, 0:B * P].rearrange("p (b d) -> p b d", b=B),
                                            f32(QT_hi[:, :, :]), ALU.subtract).then_inc(QT_lo_ready, 1)
                    nc.vector.tensor_tensor(Q_sp[:, :, 1, :], work_ps[0][:, B * P:2 * B * P].rearrange("p (b d) -> p b d", b=B),
                                            f32(Q_sp[:, :, 0, :]), ALU.subtract).then_inc(Q_lo_ready, 1)
                if n == PREP + ST_BIAS:
                    dve.wait_ge(prep_mm, ST_BIAS + 1)
                    dve.wait_ge(l3_in[0], 16 * 7)
                    nc.vector.tensor_tensor(cb_row[:, :, :], work_ps[1][:, 0:B * P].rearrange("p (b d) -> p b d", b=B),
                                            row_bias[:, 0:1, 0, :].to_broadcast([P, B, P]), ALU.add).then_inc(cb_row_ready, 1)
                for b in range(B):
                    if n == PREP + ST_UGT0 + b:
                        dve.wait_ge(upgateT_hi_ready, b + 1)
                        nc.vector.tensor_tensor(upgateT_lo[:, b, :], work_ps[b][:, :], f32(upgateT_hi[:, b, :]),
                                                ALU.subtract).then_inc(upgateT_lo_ready, 1)
                if n == PREP + ST_DNT:
                    dve.wait_ge(downT_hi_ready, 1)
                    for b in range(B):
                        nc.vector.tensor_tensor(downT_sp[:, b, :, 1, :],
                                                work_ps[0][:, b * HC * P:(b + 1) * HC * P].rearrange("p (c d) -> p c d", c=HC),
                                                f32(downT_sp[:, b, :, 0, :]), ALU.subtract).then_inc(downT_lo_ready, 1)
                for b in range(B):
                    if n == PREP + ST_R0 + b:
                        dve.wait_ge(R_hi_ready, b + 1)
                        nc.vector.tensor_tensor(R_lo[:, b, :], work_ps[1 - b][:, :], f32(R_hi[:, b, :]),
                                                ALU.subtract).then_inc(R_lo_ready, 1)

            def hid_high(n):
                dve.wait_ge(hid_ready, n + 1)
                dve.wait_ge(hid_hi_ready, n)
                if n >= RING:
                    dve.wait_ge(down_done, n - RING + 1)
                nc.vector.tensor_copy(hid_hi[:, n % RING, :], hid[:, n % RING, :]).then_inc(hid_hi_ready, 1)

            def hid_low(n):
                dve.wait_ge(hid_hi_ready, n + 1)
                if n >= RING:
                    dve.wait_ge(down_done, n - RING + 1)
                nc.vector.tensor_tensor(hid_lo[:, n % RING, :], hid[:, n % RING, :], f32(hid_hi[:, n % RING, :]),
                                        ALU.subtract).then_inc(hid_lo_ready, 1)

            def split_x1(u):
                dve.wait_ge(x1_hi_ready, u + 1)
                nc.vector.tensor_tensor(x1_lo[:, u, :], acc_ps[u][:, :], f32(x1_hi[:, u, :]),
                                        ALU.subtract).then_inc(x1_lo_ready, 1)

            def tail_hid(u, c):
                dve.wait_ge(gate3_ready, HC * u + c + 1)
                dve.wait_ge(silu_ready, HC * u + c + 1)
                if u:
                    dve.wait_ge(hid3_lo_ready, c + 1)
                nc.vector.scalar_tensor_tensor(hid3[:, c, :], tail_banks(u, c)[1][:, :],
                                               ug_bias[:, u, HC + c:HC + c + 1], silu[:, c, :],
                                               ALU.add, ALU.mult).then_inc(hid3_ready, 1)

            def tail_hid_hi(u, c):
                dve.wait_ge(hid3_ready, HC * u + c + 1)
                nc.vector.tensor_copy(hid3_hi[:, u, c, :], hid3[:, c, :]).then_inc(hid3_hi_ready, 1)

            def tail_hid_lo(u, c):
                dve.wait_ge(hid3_hi_ready, HC * u + c + 1)
                if (u, c) == (1, 1):
                    dve.wait_ge(hid3_lo_ready, HC + 1)
                nc.vector.tensor_tensor(hid3_lo[:, u, c, :], hid3[:, c, :], f32(hid3_hi[:, u, c, :]),
                                        ALU.subtract).then_inc(hid3_lo_ready, 1)

            def tail_low_order(k):
                dve.wait_ge(out_ready, k + 1)
                if k == 0:
                    dve.wait_ge(out_bias_ready, B)
                u = k // PAIR
                nc.vector.tensor_tensor(corr(k), out_bank(u, k % PAIR)[:, :, 1, :],
                                        out_bias[:, u, :].unsqueeze(1).to_broadcast([P, PAIR, D]),
                                        ALU.add).then_inc(corr_ready, 1)

            def tail_result(k):
                dve.wait_ge(corr_ready, k + 1)
                u, cols = k // PAIR, slice(k % PAIR * PAIR * D, (k % PAIR + 1) * PAIR * D)
                nc.vector.tensor_tensor(result[:, u, cols].rearrange("p (j d) -> p j d", d=D),
                                        out_bank(u, k % PAIR)[:, :, 0, :], corr(k),
                                        ALU.add).then_inc(result_ready, 1)

            def hidden(n):
                s, b, c = step_parts(n)
                dve.wait_ge(gelu_ready, n + 1)
                dve.wait_ge(up_ready, n + 1)
                if s == 0:
                    op = nc.vector.tensor_tensor(hid[:, n % RING, :], up_ps[n % 2][:, :], gelu[:, n % 2, :], ALU.mult)
                else:
                    k = (s - 1) % TOP
                    if n == B * C:
                        dve.wait_ge(route_step, B + ROUTE_STEPS)
                    op = nc.vector.scalar_tensor_tensor(hid[:, n % RING, :], up_ps[n % 2][:, :], w_route[:, b, k:k + 1],
                                                        gelu[:, n % 2, :], ALU.mult, ALU.mult)
                op.then_inc(hid_ready, 1)

            for n in range(STEPS):
                hidden(n)
                if n == 0:
                    split_x(1)
                if n == STEPS - 1:
                    hid_high(n)
                if n == PREP + ST_A:
                    leave_work_banks(n)
                if n:
                    hid_low(n - 1)
                prepare(n)
                if n > PREP + ST_Q:
                    leave_work_banks(n - 1)
                if n == X1_STEP:
                    split_x1(0)
            hid_low(STEPS - 1)
            tail_hid(0, 0)
            tail_hid_hi(0, 0)
            tail_hid_lo(0, 0)
            split_x1(1)
            tail_hid(0, 1)
            tail_hid_lo(0, 1)
            tail_hid(1, 0)
            tail_hid_hi(1, 0)
            tail_hid(1, 1)
            tail_low_order(0)
            tail_low_order(1)
            tail_hid_lo(1, 1)
            tail_result(0)
            tail_result(1)
            tail_low_order(2)
            tail_low_order(3)
            tail_result(2)
            tail_result(3)

        @block.tensor
        def _(pe):
            def product(dst, w_pair, v_pair, start, stop):
                nc.tensor.matmul(dst, w_pair[0], v_pair[0], start=start, stop=False)
                nc.tensor.matmul(dst, w_pair[1], v_pair[0], start=False, stop=False)
                return nc.tensor.matmul(dst, w_pair[0], v_pair[1], start=False, stop=stop)

            def turn_x(b):
                pe.wait_ge(x_in[b][0], 16)
                for j in range(J):
                    if b == 0 and j == J // 2:
                        pe.wait_ge(x_in[0][1], 16)
                    last = nc.tensor.matmul(acc_ps[b][:, j * P:(j + 1) * P], x_tok[:, b, j * P:(j + 1) * P], ident[:, :],
                                            is_transpose=True, start=j == 0, stop=j == J - 1)
                last.then_inc(xT_ready, 1)

            def hidden(n):
                s, b, c = step_parts(n)
                xT = (xT_hi[:, b, :], xT_lo[:, b, :])
                cols = slice(c * P, (c + 1) * P)
                for m, banks, read, done in ((GATE, gate_ps, gelu_ready, gate_ready), (UP, up_ps, hid_ready, up_ready)):
                    dst, w = banks[n % 2][:, :], (w_hi[:, s, m, cols], w_lo[:, s, m, cols])
                    parts = 1 if s or c == 0 else 2
                    if n >= 2:
                        pe.wait_ge(read, n - 1)
                    if c < 2:
                        pe.wait_ge(w_hi_ready[s][m], parts)
                    nc.tensor.matmul(dst, w[0], xT[0], start=True, stop=False)
                    if c < 2:
                        pe.wait_ge(w_lo_ready[s][m], parts)
                    nc.tensor.matmul(dst, w[1], xT[0], start=False, stop=False)
                    if c == 0 and s == 0:
                        pe.wait_ge(xT_lo_ready, b + 1)
                    nc.tensor.matmul(dst, w[0], xT[1], start=False, stop=True).then_inc(done, 1)

            def down(n):
                s, b, c = step_parts(n)
                cols = slice(c * P, (c + 1) * P)
                if c == 0:
                    pe.wait_ge(w_hi_ready[s][DOWN], 1)
                    pe.wait_ge(w_lo_ready[s][DOWN], 1)
                if n in (0, C):
                    pe.wait_ge(xT_lo_ready, b + 1)
                closes = n + 1 in (FIRST_STEPS, STEPS)
                w_h, w_l = w_hi[:, s, DOWN, cols], w_lo[:, s, DOWN, cols]
                pe.wait_ge(hid_hi_ready, n + 1)
                nc.tensor.matmul(acc_ps[b][:, :], w_h, hid_hi[:, n % RING, :], start=False, stop=False,
                                 skip_group_check=True)
                nc.tensor.matmul(acc_ps[b][:, :], w_l, hid_hi[:, n % RING, :], start=False, stop=False,
                                 skip_group_check=True)
                pe.wait_ge(hid_lo_ready, n + 1)
                nc.tensor.matmul(acc_ps[b][:, :], w_h, hid_lo[:, n % RING, :], start=False,
                                 stop=closes, skip_group_check=True).then_inc(down_done, 1)

            def prepare(n):
                if n == PREP + ST_BS:
                    pe.wait_ge(l1_in, 16 * 4)
                    pe.wait_ge(bs_mix_ready, B)
                    for b in range(B):
                        last = nc.tensor.transpose(work_ps[0][:, b * P:(b + 1) * P],
                                                   bs_mix[:, b, :, :].rearrange("o e r -> o (e r)"), ident[:, :])
                    last.then_inc(prep_mm, 1)
                if n == PREP + ST_A:
                    pe.wait_ge(bsT_ready, 1)
                    for b in range(B):
                        nc.tensor.matmul(work_ps[1][:, b * P:(b + 1) * P], bsT[:, b, :], as_sb[:, :], start=True, stop=True)
                    pe.wait_ge(masked_ready, 1)
                    for b in range(B):
                        last = nc.tensor.transpose(work_ps[0][:, (B + b) * P:(B + b + 1) * P], mix_acc[:, b, :], ident[:, :])
                    last.then_inc(prep_mm, 1)
                if n == PREP + ST_Q:
                    pe.wait_ge(A2_ready, 1)
                    pe.wait_ge(A1T_ready, 1)
                    for b in range(B):
                        nc.tensor.matmul(work_ps[0][:, b * P:(b + 1) * P], A2[:, b, :], A1T[:, b, :], start=True, stop=True)
                    for b in range(B):
                        last = nc.tensor.matmul(work_ps[0][:, (B + b) * P:(B + b + 1) * P], A1T[:, b, :], A2[:, b, :],
                                                start=True, stop=True)
                    last.then_inc(prep_mm, 1)
                if n == PREP + ST_BIAS:
                    pe.wait_ge(b1_wide_ready, 1)
                    nc.tensor.matmul(work_ps[1][:, 0:B * P], b1_wide[:, :], A2[:, :, :].rearrange("p b d -> p (b d)"),
                                     start=True, stop=True).then_inc(prep_mm, 1)
                if n in (PREP + ST_UGT0, PREP + ST_UGT1):
                    b = n - PREP - ST_UGT0
                    pe.wait_ge(l3_in[b], 16 * 7)
                    if b == 0:
                        pe.wait_ge(QT_lo_ready, 1)
                        pe.wait_ge(Q_lo_ready, 1)
                    else:
                        pe.wait_ge(cb_row_ready, 1)
                    for k in range(2 * HC):
                        last = nc.tensor.transpose(work_ps[b][:, k * P:(k + 1) * P], upgate_raw[:, b, k, :], ident[:, :])
                    last.then_inc(prep_mm, 1)
                if n == PREP + ST_DNT:
                    pe.wait_ge(upgateT_lo_ready, 1)
                    for b in range(B):
                        for c in range(HC):
                            k = b * HC + c
                            last = nc.tensor.transpose(work_ps[0][:, k * P:(k + 1) * P], down_raw[:, b, :, c], ident[:, :])
                    last.then_inc(prep_mm, 1)
                if n in (PREP + ST_R0, PREP + ST_R1):
                    b = n - PREP - ST_R0
                    pe.wait_ge(upgateT_lo_ready, B)
                    if b == 1:
                        pe.wait_ge(downT_lo_ready, B)
                    product(work_ps[1 - b][:, :], (QT_hi[:, b, :], QT_lo[:, b, :]), (upgateT_hi[:, b, :], upgateT_lo[:, b, :]),
                            True, True).then_inc(prep_mm, 1)

            def tail_up_gate(u, c):
                up, gate = tail_banks(u, c)
                x1 = (x1_hi[:, u, :], x1_lo[:, u, :])
                if c == 0:
                    pe.wait_ge(x1_hi_ready, u + 1)
                    pe.wait_ge(x1_lo_ready, u + 1)
                if (u, c) == (0, 0):
                    pe.wait_ge(R_lo_ready, B)
                if (u, c) == (0, 1):
                    pe.wait_ge(gelu_ready, STEPS - 1)
                    pe.wait_ge(hid_ready, STEPS - 1)
                if (u, c) == (1, 0):
                    pe.wait_ge(gelu_ready, STEPS)
                if (u, c) == (1, 1):
                    pe.wait_ge(hid3_ready, 1)
                for dst, k, done in ((up, c, up3_ready), (gate, HC + c, gate3_ready)):
                    cols = slice(k * P, (k + 1) * P)
                    product(dst[:, :], (R_hi[:, u, cols], R_lo[:, u, cols]), x1, True, True).then_inc(done, 1)

            def out_tiles(u, v_hi, v_lo, w_sp, start, stop, ready=None):
                for j in range(J):
                    k, first, last = j // PAIR, j % PAIR == 0, j % PAIR == PAIR - 1
                    tile, cols = out_bank(u, k)[:, j % PAIR, :, :], slice(j * P, (j + 1) * P)
                    nc.tensor.matmul(tile, v_hi[:, cols], w_sp, start=start and first, stop=False)
                    mm = nc.tensor.matmul(tile[:, 1, :], v_lo[:, cols], w_sp[:, 0, :], start=False, stop=stop and last)
                    if ready and last:
                        mm.then_inc(ready, 1)

            def tail_residual(u):
                if u == 0:
                    pe.wait_ge(Q_lo_ready, 1)
                    pe.wait_ge(x1_lo_ready, 1)
                    pe.wait_ge(hid_ready, STEPS)
                else:
                    pe.wait_ge(hid3_ready, 2)
                out_tiles(u, x1_hi[:, u, :], x1_lo[:, u, :], Q_sp[:, u, :, :], True, False)

            def tail_down(u, c):
                pe.wait_ge(hid3_hi_ready, HC * u + c + 1)
                pe.wait_ge(hid3_lo_ready, HC * u + c + 1)
                if (u, c) == (0, 0):
                    pe.wait_ge(downT_lo_ready, B)
                end = c == HC - 1
                out_tiles(u, hid3_hi[:, u, c, :], hid3_lo[:, u, c, :], downT_sp[:, u, c, :, :], False, end,
                          out_ready if end else None)

            def warm_up(count):
                for _ in range(count):
                    nc.tensor.matmul(gate_ps[1][:, :].rearrange("p (j d) -> p j d", j=J), zeros[:, :],
                                     zeros[:, :].unsqueeze(1).to_broadcast([P, J, P]), start=True, stop=True)

            pe.wait_ge(zeros_ready, 1)
            warm_up(WARM_BEFORE_X)
            pe.wait_ge(ident_ready, 1)
            turn_x(0)
            warm_up(WARM_AFTER_X)
            pe.wait_ge(xT_hi_ready, 1)
            for n in range(STEPS):
                hidden(n)
                if n == 0:
                    turn_x(1)
                if n >= LAG:
                    down(n - LAG)
                prepare(n)
            tail_up_gate(0, 0)
            tail_residual(0)
            down(STEPS - 2)
            down(STEPS - 1)
            tail_up_gate(0, 1)
            tail_down(0, 0)
            tail_up_gate(1, 0)
            tail_up_gate(1, 1)
            tail_down(0, 1)
            tail_residual(1)
            tail_down(1, 0)
            tail_down(1, 1)


_INS = ['x', 'cond_8', 'L0_cond_skill_gate', 'L0_cond_skill_up', 'L0_cond_skill_down', 'L0_cond_shared_gate',
        'L0_cond_shared_up', 'L0_cond_shared_down', 'L1_cond_W_base', 'L1_cond_b_base', 'L1_cond_As', 'L1_cond_Bs',
        'L2_cond_weight', 'L2_cond_mask', 'L2_cond_bias', 'L3_cond_W_up', 'L3_cond_b_up', 'L3_cond_W_gate',
        'L3_cond_b_gate', 'L3_cond_W_down', 'L3_cond_b_down']


def kernel(**inputs):
    import numpy as _np
    import concourse.bacc as _bacc
    from concourse import mybir as _mybir
    from concourse.bass_utils import run_bass_kernel_spmd as _run

    nc = _bacc.Bacc("TRN2", target_bir_lowering=False, num_devices=1)
    arrays, args = {}, []
    for name in _INS:
        a = _np.ascontiguousarray(inputs[name])
        arrays[f"in_{name}_dram"] = a
        args.append(nc.dram_tensor(f"in_{name}_dram", a.shape, _mybir.dt.from_np(a.dtype), kind="ExternalInput").ap())
    out = nc.dram_tensor("out_0_dram", inputs["x"].shape, _mybir.dt.from_np(_np.dtype("float32")), kind="ExternalOutput").ap()
    build(nc, *args, out)
    r = _run(nc, [arrays], core_ids=[0])
    return r.results[0]["out_0_dram"]
```
